# Optimizing a Trainium2 kernel written in Bass

```python
import numpy as np
import jax
import jax.numpy as jnp

def _softmax(x, axis=-1):
    return jax.nn.softmax(x, axis=axis)

def _gelu(x):
    return jax.nn.gelu(x, approximate=True)

def _silu(x):
    return jax.nn.silu(x)

def _sigmoid(x):
    return jax.nn.sigmoid(x)

def _layernorm(x, axis=-1, eps=1e-05):
    m = jnp.mean(x, axis=axis, keepdims=True)
    v = jnp.var(x, axis=axis, keepdims=True)
    return (x - m) / jnp.sqrt(v + eps)

def _scatter_add(tgt, idx, src, axis=0):
    return tgt.at[idx].add(src)

def _segment_sum(src, seg, n):
    return jax.ops.segment_sum(src, seg, n)
kernel_name = 'mk_hybrid_d1_jaxref_r8_1a0be8'

def setup_inputs(seed: int=0):
    np.random.seed(seed)
    _w = jnp.asarray

    def _L0_attn_a_setup():
        import jax, jax.numpy as jnp
        import numpy as np
        B, T, C = (2, 256, 128)
        NHEADS = 16
        HEAD_DIM = C // NHEADS
        THETA = 10000.0
        SCALE_BASE = 512.0
        GN_EPS = 1e-05

        def _rotate_half(x):
            x1 = x[..., 0::2]
            x2 = x[..., 1::2]
            return jnp.stack([-x2, x1], axis=-1).reshape(x.shape)

        def _rope_xpos(q, k, T):
            d = q.shape[-1]
            half = jnp.arange(0, d, 2, dtype=jnp.float32)
            inv_freq = 1.0 / THETA ** (half / d)
            t = jnp.arange(T, dtype=jnp.float32)
            freqs = t[:, None] * inv_freq[None, :]
            freqs = jnp.repeat(freqs, 2, axis=-1)
            scale_vec = (half + 0.4 * d) / (1.4 * d)
            power = (t - T // 2) / SCALE_BASE
            scale = scale_vec[None, :] ** power[:, None]
            scale = jnp.repeat(scale, 2, axis=-1)
            cos, sin = (jnp.cos(freqs), jnp.sin(freqs))
            q = q * (cos * scale) + _rotate_half(q) * (sin * scale)
            k = k * (cos / scale) + _rotate_half(k) * (sin / scale)
            return (q, k)

        def _decay_mask(T):
            gamma = 1.0 - 2.0 ** (-5.0 - jnp.arange(NHEADS, dtype=jnp.float32))
            idx = jnp.arange(T)
            diff = idx[:, None] - idx[None, :]
            causal = diff >= 0
            expn = jnp.where(causal, diff, 0).astype(jnp.float32)
            return jnp.where(causal[None], gamma[:, None, None] ** expn[None], 0.0)
        key = jax.random.key(seed)
        ks = jax.random.split(key, 4)
        s = 0.02
        return {'x': jax.random.normal(ks[0], (B, T, C), jnp.float32), 'w_qkv': jax.random.normal(ks[1], (3 * C, C), jnp.float32) * s, 'w_gated': jax.random.normal(ks[2], (C, C), jnp.float32) * s, 'w_proj': jax.random.normal(ks[3], (C, C), jnp.float32) * s, 'gn_weight': jnp.ones((C,), jnp.float32), 'gn_bias': jnp.zeros((C,), jnp.float32)}
    _L0_attn_a_in = _L0_attn_a_setup()

    def _L0_attn_b_setup():
        import math
        import jax, jax.numpy as jnp
        import numpy as np
        EMBED_DIM = 128
        NDIM = 16
        SEQ = 512
        BATCH = 8
        SCALE = math.sqrt(1.0 / NDIM)
        DT_MIN, DT_MAX = (0.001, 0.1)

        def _ssm_kernel(log_dt, log_A_real, A_imag, B, C, L):
            dt = jnp.exp(log_dt)
            A = -jnp.exp(log_A_real) + 1j * A_imag
            Bc = B[..., 0] + 1j * B[..., 1]
            Cc = C[..., 0] + 1j * C[..., 1]
            dtA = dt * A
            dA = (1.0 + dtA / 2) / (1.0 - dtA / 2)
            CB = Cc * Bc * dt / (1.0 - dtA / 2)
            powers = jnp.exp(jnp.log(dA)[:, :, None] * jnp.arange(L, dtype=jnp.float32))
            K = 2.0 * jnp.einsum('hn,hnl->hl', CB, powers).real
            return K * SCALE
        key = jax.random.key(seed)
        ks = jax.random.split(key, 6)
        x = jax.random.normal(ks[0], (SEQ, BATCH, EMBED_DIM), jnp.float32)
        log_dt = jax.random.uniform(ks[1], (EMBED_DIM, 1), jnp.float32) * (math.log(DT_MAX) - math.log(DT_MIN)) + math.log(DT_MIN)
        log_A_real = jnp.log(0.5 * jnp.ones((EMBED_DIM, NDIM), jnp.float32))
        A_imag = jnp.tile(math.pi * jnp.arange(NDIM, dtype=jnp.float32)[None, :], (EMBED_DIM, 1))
        B = 0.5 * jax.random.normal(ks[2], (EMBED_DIM, NDIM, 2), jnp.float32)
        C = jax.random.normal(ks[3], (EMBED_DIM, NDIM, 2), jnp.float32)
        D = jax.random.normal(ks[4], (EMBED_DIM,), jnp.float32)
        return dict(x=x, log_dt=log_dt, log_A_real=log_A_real, A_imag=A_imag, B=B, C=C, D=D)
    _L0_attn_b_in = _L0_attn_b_setup()

    def _L0_ffn_setup():
        import jax, jax.numpy as jnp
        import numpy as np
        B, S, D, F, E, K = (4, 256, 128, 512, 4, 2)
        key = jax.random.key(seed)
        k = jax.random.split(key, 6)
        x = jax.random.normal(k[0], (B, S, D), jnp.float32)
        router_w = jax.random.normal(k[1], (D, E), jnp.float32) * D ** (-0.5)
        router_b = jnp.zeros((E,), jnp.float32)
        w1 = jax.random.normal(k[2], (E, D, F), jnp.float32) * 0.02
        w3 = jax.random.normal(k[3], (E, D, F), jnp.float32) * 0.02
        w2 = jax.random.normal(k[4], (E, F, D), jnp.float32) * 0.02
        return {'x': x, 'router_w': router_w, 'router_b': router_b, 'w1': w1, 'w3': w3, 'w2': w2}
    _L0_ffn_in = _L0_ffn_setup()
    _d = {'L0_attn_a_x': _L0_attn_a_in['x'], 'L0_attn_a_w_qkv': _L0_attn_a_in['w_qkv'], 'L0_attn_a_w_gated': _L0_attn_a_in['w_gated'], 'L0_attn_a_w_proj': _L0_attn_a_in['w_proj'], 'L0_attn_a_gn_weight': _L0_attn_a_in['gn_weight'], 'L0_attn_a_gn_bias': _L0_attn_a_in['gn_bias'], 'L0_attn_b_log_dt': _L0_attn_b_in['log_dt'], 'L0_attn_b_log_A_real': _L0_attn_b_in['log_A_real'], 'L0_attn_b_A_imag': _L0_attn_b_in['A_imag'], 'L0_attn_b_B': _L0_attn_b_in['B'], 'L0_attn_b_C': _L0_attn_b_in['C'], 'L0_attn_b_D': _L0_attn_b_in['D'], 'L0_ffn_router_w': _L0_ffn_in['router_w'], 'L0_ffn_router_b': _L0_ffn_in['router_b'], 'L0_ffn_w1': _L0_ffn_in['w1'], 'L0_ffn_w3': _L0_ffn_in['w3'], 'L0_ffn_w2': _L0_ffn_in['w2']}
    _x0 = _d['L0_attn_a_x']
    _d['L0_attn_a_x'] = jax.random.normal(jax.random.fold_in(jax.random.key(seed), 1), (8, 512, 128), dtype=_x0.dtype)
    del _x0
    return _d

def reference(L0_attn_a_x, L0_attn_a_w_qkv, L0_attn_a_w_gated, L0_attn_a_w_proj, L0_attn_a_gn_weight, L0_attn_a_gn_bias, L0_attn_b_log_dt, L0_attn_b_log_A_real, L0_attn_b_A_imag, L0_attn_b_B, L0_attn_b_C, L0_attn_b_D, L0_ffn_router_w, L0_ffn_router_b, L0_ffn_w1, L0_ffn_w3, L0_ffn_w2):

    def _L0_attn_a_ref(x, w_qkv, w_gated, w_proj, gn_weight, gn_bias):
        import jax, jax.numpy as jnp
        import numpy as np
        B, T, C = (2, 256, 128)
        NHEADS = 16
        HEAD_DIM = C // NHEADS
        THETA = 10000.0
        SCALE_BASE = 512.0
        GN_EPS = 1e-05

        def _rotate_half(x):
            x1 = x[..., 0::2]
            x2 = x[..., 1::2]
            return jnp.stack([-x2, x1], axis=-1).reshape(x.shape)

        def _rope_xpos(q, k, T):
            d = q.shape[-1]
            half = jnp.arange(0, d, 2, dtype=jnp.float32)
            inv_freq = 1.0 / THETA ** (half / d)
            t = jnp.arange(T, dtype=jnp.float32)
            freqs = t[:, None] * inv_freq[None, :]
            freqs = jnp.repeat(freqs, 2, axis=-1)
            scale_vec = (half + 0.4 * d) / (1.4 * d)
            power = (t - T // 2) / SCALE_BASE
            scale = scale_vec[None, :] ** power[:, None]
            scale = jnp.repeat(scale, 2, axis=-1)
            cos, sin = (jnp.cos(freqs), jnp.sin(freqs))
            q = q * (cos * scale) + _rotate_half(q) * (sin * scale)
            k = k * (cos / scale) + _rotate_half(k) * (sin / scale)
            return (q, k)

        def _decay_mask(T):
            gamma = 1.0 - 2.0 ** (-5.0 - jnp.arange(NHEADS, dtype=jnp.float32))
            idx = jnp.arange(T)
            diff = idx[:, None] - idx[None, :]
            causal = diff >= 0
            expn = jnp.where(causal, diff, 0).astype(jnp.float32)
            return jnp.where(causal[None], gamma[:, None, None] ** expn[None], 0.0)
        Bx, Tx, Cx = x.shape
        qkv = x @ w_qkv.T
        q, k, v = jnp.split(qkv, 3, axis=-1)

        def to_heads(u):
            return u.reshape(Bx, Tx, NHEADS, HEAD_DIM).transpose(0, 2, 1, 3)
        q, k, v = (to_heads(q), to_heads(k), to_heads(v))
        q, k = _rope_xpos(q, k, Tx)
        mask = _decay_mask(Tx)
        scores = jnp.einsum('bhtd,bhsd->bhts', q, k) * HEAD_DIM ** (-0.5)
        scores = scores * mask[None]
        y = jnp.einsum('bhts,bhsd->bhtd', scores, v)
        y = y.transpose(0, 2, 1, 3).reshape(Bx, Tx, Cx)
        yt = y.transpose(0, 2, 1).reshape(Bx, NHEADS, HEAD_DIM, Tx)
        mean = yt.mean(axis=(2, 3), keepdims=True)
        var = yt.var(axis=(2, 3), keepdims=True)
        yn = (yt - mean) / jnp.sqrt(var + GN_EPS)
        yn = yn.reshape(Bx, Cx, Tx)
        yn = yn * gn_weight[None, :, None] + gn_bias[None, :, None]
        yn = yn.transpose(0, 2, 1)
        out = jax.nn.silu(x @ w_gated.T) * yn
        return out @ w_proj.T

    def _L0_attn_b_ref(x, log_dt, log_A_real, A_imag, B, C, D):
        import math
        import jax, jax.numpy as jnp
        import numpy as np
        EMBED_DIM = 128
        NDIM = 16
        SEQ = 512
        BATCH = 8
        SCALE = math.sqrt(1.0 / NDIM)
        DT_MIN, DT_MAX = (0.001, 0.1)

        def _ssm_kernel(log_dt, log_A_real, A_imag, B, C, L):
            dt = jnp.exp(log_dt)
            A = -jnp.exp(log_A_real) + 1j * A_imag
            Bc = B[..., 0] + 1j * B[..., 1]
            Cc = C[..., 0] + 1j * C[..., 1]
            dtA = dt * A
            dA = (1.0 + dtA / 2) / (1.0 - dtA / 2)
            CB = Cc * Bc * dt / (1.0 - dtA / 2)
            powers = jnp.exp(jnp.log(dA)[:, :, None] * jnp.arange(L, dtype=jnp.float32))
            K = 2.0 * jnp.einsum('hn,hnl->hl', CB, powers).real
            return K * SCALE
        L = x.shape[0]
        k = _ssm_kernel(log_dt, log_A_real, A_imag, B, C, L)
        u = jnp.transpose(x, (1, 2, 0))
        n = 2 * L
        y = jnp.fft.irfft(jnp.fft.rfft(u, n=n) * jnp.fft.rfft(k, n=n), n=n)[..., :L]
        y = y + u * D[None, :, None]
        return jnp.transpose(y, (2, 0, 1))

    def _L0_ffn_ref(x, router_w, router_b, w1, w3, w2):
        import jax, jax.numpy as jnp
        import numpy as np
        B, S, D, F, E, K = (4, 256, 128, 512, 4, 2)
        b, s, d = x.shape
        T = b * s
        e = router_w.shape[1]
        xf = x.reshape(T, d)
        logits = xf @ router_w + router_b
        probs = jax.nn.softmax(logits, axis=-1)
        top_p, top_i = jax.lax.top_k(probs, K)
        top_p = top_p / jnp.sum(top_p, axis=-1, keepdims=True)
        gates = jnp.zeros((T, e), xf.dtype).at[jnp.arange(T)[:, None], top_i].add(top_p)
        h = jax.nn.silu(jnp.einsum('td,edf->etf', xf, w1)) * jnp.einsum('td,edf->etf', xf, w3)
        expert_out = jnp.einsum('etf,efd->etd', h, w2)
        out = jnp.einsum('te,etd->td', gates, expert_out)
        return out.reshape(b, s, d)
    x = L0_attn_a_x
    x = x + _L0_attn_a_ref(_layernorm(x, axis=-1), L0_attn_a_w_qkv, L0_attn_a_w_gated, L0_attn_a_w_proj, L0_attn_a_gn_weight, L0_attn_a_gn_bias)
    x = x + _L0_ffn_ref(_layernorm(x, axis=-1), L0_ffn_router_w, L0_ffn_router_b, L0_ffn_w1, L0_ffn_w3, L0_ffn_w2)
    x = x + _L0_attn_b_ref(_layernorm(x, axis=-1), L0_attn_b_log_dt, L0_attn_b_log_A_real, L0_attn_b_A_imag, L0_attn_b_B, L0_attn_b_C, L0_attn_b_D)
    x = x + _L0_ffn_ref(_layernorm(x, axis=-1), L0_ffn_router_w, L0_ffn_router_b, L0_ffn_w1, L0_ffn_w3, L0_ffn_w2)
    return x

_drawn_inputs = setup_inputs


def setup_inputs(seed=0):
    import zlib

    import numpy as np

    out = dict(_drawn_inputs(seed))
    spreads = {'L0_attn_a_gn_weight': (1.0, 0.6),
     'L0_attn_a_gn_bias': (0.0, 0.8),
     'L0_attn_b_log_A_real': (-0.6931471824645996, 0.6),
     'L0_ffn_router_b': (0.0, 0.8)}
    factors = {'L0_ffn_router_w': 6.244, 'L0_ffn_w1': 4.667, 'L0_ffn_w3': 4.638, 'L0_ffn_w2': 4.629}
    for name, (base, spread) in spreads.items():
        noise = np.random.default_rng([zlib.crc32(name.encode()), seed]).standard_normal(out[name].shape)
        drawn = base * np.exp(spread * noise) if base else spread * noise
        out[name] = jnp.asarray(drawn.astype(out[name].dtype))
    for name, factor in factors.items():
        out[name] = (out[name] * factor).astype(out[name].dtype)
    return out
```

```python
from contextlib import ExitStack

import numpy as np

import concourse.bass as bass
from concourse import mybir

F32 = mybir.dt.float32
F32R = mybir.dt.float32r
ALU = mybir.AluOpType
ACT = mybir.ActivationFunctionType
AX_X = mybir.AxisListType.X

P = 128
B, T, C = 8, 512, 128
NC = T // P
H, HD = 16, 8
HG = 4
E, F = 4, 512
FC = F // P
NCH = E * FC
NS = 16
EPS = 1e-5


def constants():
    d = np.arange(0, HD, 2, dtype=np.float64)
    inv_freq = 1.0 / 10000.0 ** (d / HD)
    t = np.arange(T, dtype=np.float64)
    scale = ((d + 0.4 * HD) / (1.4 * HD))[:, None] ** ((t - T // 2) / 512.0)[None, :]
    cos, sin = np.cos(inv_freq[:, None] * t), np.sin(inv_freq[:, None] * t)
    gamma = 1.0 - 2.0 ** (-5.0 - np.arange(H, dtype=np.float64))
    rope = np.zeros((C, 4, T))
    for c in range(C):
        h, i, odd = c // HD, c % HD // 2, c % 2
        sign = 1.0 if odd else -1.0
        up, down = gamma[h] ** t * HD ** -0.5, gamma[h] ** -t
        rope[c] = (cos[i] * scale[i] * up, sign * sin[i] * scale[i] * up,
                   cos[i] / scale[i] * down, sign * sin[i] / scale[i] * down)
    i = np.arange(P)
    head = i // HD
    same = (head[:, None] == head[None, :]).astype(np.float64)
    causal = np.broadcast_to((i[:, None] <= i[None, :]).astype(np.float64)[:, None, :], (P, HG, P))
    onehot = (head[:, None] == np.arange(H)[None, :]).astype(np.float64)
    lower = np.broadcast_to(np.tril(np.ones((E, E)), -1), (P, NC, E, E))
    tables = {
        "rope": rope, "causal": causal, "same_head": same, "head_mean": same / HD,
        "onehot": onehot, "ident": np.eye(P), "lower": lower,
    }
    return {n: np.ascontiguousarray(a, dtype=np.float32) for n, a in tables.items()}


class Own:

    def __init__(self, eng, sem):
        self.eng, self.sem, self.base, self.k = eng, sem, 0, 0

    def did(self, ins):
        ins.then_inc(self.sem, 1)
        self.k += 1

    def link(self, ins):
        self.did(ins)
        self.wait()

    def wait(self, back=0):
        self.eng.wait_ge(self.sem, self.base + self.k - back)


def steps(eng, own, first, step, last, per):
    first()
    k0 = own.k if own else 0
    with eng.Fori(0, (B - 2) // 2) as j:
        if own:
            own.base, own.k = k0 + j * (2 * per), 0
        step(2 * j + 1, 1)
        step(2 * j + 2, 0)
        if own:
            assert own.k == 2 * per, (own.k, per)
    if own:
        own.base, own.k = 0, k0 + (B - 2) * per
    last()


def build(nc, x, w5, wv, wp, gn, log_dt, log_a, a_im, bc, cc, dd, rw, rb, w1, w3, w2,
          rope, causal, same_head, head_mean, onehot, ident, lower, out, stop=4):
    ctx = ExitStack()
    with ctx:
        def sem(name):
            return ctx.enter_context(nc.semaphore(name))

        def alloc(stack, name, shape, dt=F32):
            return stack.enter_context(nc.sbuf_tensor(name, shape, dt))

        bank = [ctx.enter_context(nc.psum_tensor(f"bank{i}", [P, 512], F32)) for i in range(8)]
        gate_rows = nc.dram_tensor("gate_rows", (2, 2, P * NC * E), F32, kind="Internal").ap()

        X = alloc(ctx, "X", [P, B, NC, C])
        W1 = [alloc(ctx, f"W1{s}", [P, E, F], F32R) for s in ("hi", "lo")]
        W3 = [alloc(ctx, f"W3{s}", [P, E, F], F32R) for s in ("hi", "lo")]
        ID = alloc(ctx, "ID", [P, P])
        stats = alloc(ctx, "stats", [P, NC, 6])
        mv = alloc(ctx, "mv", [P, NC, 2])
        veps = alloc(ctx, "veps", [P, NC])
        rstd = alloc(ctx, "rstd", [P, NC])
        half = alloc(ctx, "half", [P, 32])
        xn = alloc(ctx, "xn", [P, NC, C])
        xnT = alloc(ctx, "xnT", [P, T])
        RW = alloc(ctx, "RW", [P, E])
        RB = alloc(ctx, "RB", [P, 1, E])

        att = ExitStack()
        with att:
            Wq5 = alloc(att, "Wq5", [P, 5, C])
            Wv = alloc(att, "Wv", [P, C])
            Wp = alloc(att, "Wp", [P, C])
            RP = alloc(att, "RP", [P, 4, T])
            CAUS = alloc(att, "CAUS", [P, HG, P])
            SAME = alloc(att, "SAME", [P, P])
            HMEAN = alloc(att, "HMEAN", [P, P])
            ONEHOT = alloc(att, "ONEHOT", [P, H])
            GN = alloc(att, "GN", [P, 2])
            qT = [alloc(att, f"qT{i}", [P, T]) for i in range(2)]
            kT = [alloc(att, f"kT{i}", [P, T]) for i in range(2)]
            ktok = [alloc(att, f"ktok{i}", [P, NC, C]) for i in range(2)]
            V = [alloc(att, f"V{i}", [P, NC, C]) for i in range(2)]
            VE = [alloc(att, f"VE{i}", [P, NC, HG, C]) for i in range(2)]
            QE = [alloc(att, f"QE{i}", [P, H, T]) for i in range(2)]
            PR = alloc(att, "PR", [P, 8, HG, P])
            t1 = alloc(att, "t1", [P, T])
            t2 = alloc(att, "t2", [P, T])
            SG = [alloc(att, f"SG{i}", [P, T]) for i in range(2)]
            Ysb = alloc(att, "Ysb", [P, T])
            og = alloc(att, "og", [P, T])
            STsb = alloc(att, "STsb", [P, NC, C])
            gs6 = alloc(att, "gs6", [P, 6])
            gmv = alloc(att, "gmv", [P, 2])
            gst = alloc(att, "gst", [P, 2])
            gsm = alloc(att, "gsm", [P, 8])
        W1raw = QE[1][:, 0:4, :]
        W3raw = QE[1][:, 4:8, :]

        W2 = [alloc(ctx, f"W2{s}", [P, NCH, C], F32R) for s in ("hi", "lo")]
        xs = [[alloc(ctx, f"x{s}{i}", [P, T], F32R) for s in ("hi", "lo")] for i in range(2)]
        hs = [[alloc(ctx, f"h{s}{i}", [P, F], F32R) for s in ("hi", "lo")] for i in range(4)]
        hf = [alloc(ctx, f"hf{i}", [P, T]) for i in range(2)]
        sa = [alloc(ctx, f"sa{i}", [P, T]) for i in range(2)]
        GB = [alloc(ctx, f"GB{i}", [P, T, E]) for i in range(2)]
        oacc = [alloc(ctx, f"oacc{i}", [P, T]) for i in range(2)]
        otmp = alloc(ctx, "otmp", [P, T])
        LG = alloc(ctx, "LG", [P, NC, E])
        LD = alloc(ctx, "LD", [P, NC, E])
        LE = alloc(ctx, "LE", [P, NC, E])
        mx = alloc(ctx, "mx", [P, NC])
        GT = alloc(ctx, "GT", [P, NC, E, E])
        EQ = alloc(ctx, "EQ", [P, NC, E, E])
        LOWER = alloc(ctx, "LOWER", [P, NC, E, E])
        rank = alloc(ctx, "rank", [P, NC, E])
        pm = alloc(ctx, "pm", [P, NC, E])
        smr = alloc(ctx, "smr", [P, NC])
        G = alloc(ctx, "G", [P, NC, E])
        EULER = alloc(ctx, "EULER", [P, NS])
        xns = [alloc(ctx, f"xns{i}", [P, NC, C]) for i in range(2)]
        XT = alloc(ctx, "XT", [P, B, T])
        rows = alloc(ctx, "rows", [P, 56, NS])
        BC4 = alloc(ctx, "BC4", [P, 4, NS])
        DD = alloc(ctx, "DD", [P, 1])
        DT = alloc(ctx, "DT", [P, 1])
        L2 = alloc(ctx, "L2", [P, B, 2, NS])
        tmp = alloc(ctx, "tmp", [P, B, 2, NS])
        K = alloc(ctx, "K", [P, B])
        DK = alloc(ctx, "DK", [P, B, P])
        sst = alloc(ctx, "sst", [P, 2, NC, 6])
        smv = alloc(ctx, "smv", [P, 2, NC, 2])
        sve = alloc(ctx, "sve", [P, 2, NC])
        srs = alloc(ctx, "srs", [P, 2, NC])

        x_first, x_second, x_rest = sem("x_first"), sem("x_second"), sem("x_rest")
        att_in, w13_in, ffn_in, w2_in, par_in = (
            sem("att_in"), sem("w13_in"), sem("ffn_in"), sem("w2_in"), sem("par_in"))
        ATT_LOADS, FFN_LOADS, PAR_LOADS = 10, 3, 6
        const_set, w13_hi, w13_lo = sem("const_set"), sem("w13_hi"), sem("w13_lo")
        dve_own, pool_own = sem("dve_own"), sem("pool_own")
        a_ve, a_rs, a_xn = sem("a_variance"), sem("a_rstd"), sem("a_normed")
        KINDS = {"T": 1, "q": 1, "k": 1, "v": 1, "kt": 1, "gn": 0, "proj": 0, "qs": 0, "ks": 0, "g": 0}
        made = {kind: sem(f"made_{kind}") for kind in KINDS}
        rope_done, gn_read = sem("rope_done"), sem("gn_read")
        xnT_ready, qk_ready, v_ready, ktok_ready, sg_ready = (
            sem("xnT_ready"), sem("qk_ready"), sem("v_ready"), sem("ktok_ready"), sem("sg_ready"))
        qe_act, qe_pool, qe_dve = sem("qe_act"), sem("qe_pool"), sem("qe_dve")
        sc_ready, p_ready, pv_done = sem("sc_ready"), sem("p_ready"), sem("pv_done")
        st_ready, st_sb, y_sb = sem("st_ready"), sem("st_sb"), sem("y_sb")
        gm_ready, gv_ready, gr_ready, og_ready, x1_done = (
            sem("gm_ready"), sem("gv_ready"), sem("gr_ready"), sem("og_ready"), sem("x1_done"))
        ve_zero, w2_hi, w2_lo = sem("ve_zero"), sem("w2_hi"), sem("w2_lo")
        k_ready, dk_ready = sem("k_ready"), sem("dk_ready")
        s_ve, s_rs, s_xn, s_T, s_xT = (
            sem("s_variance"), sem("s_rstd"), sem("s_normed"), sem("s_T"), sem("s_xT"))
        s_y, x3_done = sem("s_y"), sem("x3_done")
        stored = sem("stored")

        def mixture_sems(tag):
            names = ("ve rs xn T xT xs lg lr pr pr_in le gates gst gld a b sa h hi lo o od tr xd".split())
            return {n: sem(f"m{tag}_{n}") for n in names}

        mix = [mixture_sems(1), mixture_sems(2)]

        def read_of(kind, m):
            return {"T": (xnT_ready, m + 1), "v": (v_ready, 5 * m + 5), "kt": (ktok_ready, m + 1),
                    "q": (rope_done, 4 * m + 1), "qs": (rope_done, 4 * m + 2),
                    "k": (rope_done, 4 * m + 3), "ks": (rope_done, 4 * m + 4),
                    "g": (sg_ready, m + 1), "gn": (gn_read, m + 1), "proj": (x1_done, m + 1)}[kind]

        def free_for(eng, kind, m):
            known = isinstance(m, int)
            before = {"q": "T", "k": "q", "v": "k", "kt": "v", "proj": "gn", "ks": "qs", "g": "ks"}
            if kind in before:
                eng.wait_ge(*read_of(before[kind], m))
            elif kind == "T" and not (known and m == 0):
                eng.wait_ge(*read_of("kt", m - 1))
            elif kind == "qs" and not (known and m < 2):
                eng.wait_ge(*read_of("proj", m - 2))
            elif kind == "qs" and m == 1:
                eng.wait_ge(*read_of("g", 0))
            elif kind == "gn":
                last = known and m == B - 1
                eng.wait_ge(*(read_of("proj", m - 1) if last else read_of("g", m + 1)))
            return bank[6 + KINDS[kind]]

        def ready_for(eng, kind, m):
            eng.wait_ge(made[kind], m + 1)
            return bank[6 + KINDS[kind]]

        def wait_apart(eng, semaphore, value):
            if not isinstance(value, int):
                value = eng.to_reg(value)
                eng.wait_ge(x_first, 16)
            eng.wait_ge(semaphore, value)

        block = ctx.enter_context(nc.Block())

        @block.sync
        def _(sp):
            xv = x.rearrange("b (c p) h -> p b c h", p=P)
            sp.dma_start(X[:, 0], xv[:, 0]).then_inc(x_first, 16)
            loads = [(Wq5[:], w5), (ID[:], ident), (RP[:], rope), (Wv[:], wv), (ONEHOT[:], onehot),
                     (CAUS[:], causal), (SAME[:], same_head), (HMEAN[:], head_mean), (Wp[:], wp),
                     (GN[:], gn)]
            assert len(loads) == ATT_LOADS
            for dst, src in loads:
                sp.dma_start(dst, src).then_inc(att_in, 16)
            sp.dma_start(X[:, 1], xv[:, 1]).then_inc(x_second, 16)
            for b in range(2, B):
                sp.dma_start(X[:, b], xv[:, b]).then_inc(x_rest, 16)
            sp.dma_start(W1raw, w1.rearrange("e d f -> d e f")).then_inc(w13_in, 16)
            sp.dma_start(W3raw, w3.rearrange("e d f -> d e f")).then_inc(w13_in, 16)
            sp.dma_start(RW[:], rw).then_inc(ffn_in, 16)
            sp.dma_start(RB[:, 0, :], rb.partition_broadcast(P)).then_inc(ffn_in, 16)
            sp.wait_ge(x1_done, B)
            sp.dma_start(GB[1][:].rearrange("p t e -> p (t e)").rearrange("p (k c) -> p k c", c=C),
                         w2.rearrange("e (m f) d -> f (e m) d", f=P)).then_inc(w2_in, 16)
            sp.dma_start(LOWER[:], lower).then_inc(ffn_in, 16)
            parts = [(DT[:], log_dt), (rows[:, 0], log_a), (rows[:, 1], a_im),
                     (BC4[:, 0:2], bc), (BC4[:, 2:4], cc),
                     (DD[:], dd.rearrange("(h o) -> h o", o=1))]
            for dst, src in parts:
                sp.dma_start(dst, src).then_inc(par_in, 16)
            assert len(parts) == PAR_LOADS

            def gates_out(s, m, p):
                sp.wait_ge(s["gates"], m + 1)
                row = gate_rows[0, p]
                sp.dma_start(row.rearrange("(c q e) -> q c e", c=NC, e=E), G[:]).then_inc(s["gst"], 16)
                sp.wait_ge(s["gst"], 16 * (m + 1))
                sp.dma_start(GB[p][:].rearrange("q t e -> q (t e)"),
                             row.partition_broadcast(P)).then_inc(s["gld"], 16)

            def mixture(s, final):
                if s is mix[0]:
                    sp.wait_ge(w2_lo, 1)
                gates_out(s, 0, 0)
                gates_out(s, 1, 1)
                with sp.Fori(0, (B - 2) // 2) as j:
                    gates_out(s, 2 * j + 2, 0)
                    gates_out(s, 2 * j + 3, 1)

            ov = out.rearrange("b (c p) h -> p b c h", p=P)
            if stop >= 2:
                mixture(mix[0], False)
            if stop >= 4:
                mixture(mix[1], True)
            done = {1: x1_done, 2: mix[0]["xd"], 3: x3_done, 4: mix[1]["xd"]}[stop]
            for b in range(B):
                sp.wait_ge(done, 8 if stop == 3 else b + 1)
                sp.dma_start(ov[:, b], X[:, b]).then_inc(stored, 16)
            sp.wait_ge(stored, 16 * B)

        @block.tensor
        def _(pe):
            def front_T(m, p):
                pe.wait_ge(a_xn, m + 1)
                ps = free_for(pe, "T", m)
                for c in range(NC):
                    mm = pe.transpose(ps[:, c * P:(c + 1) * P], xn[:, c, :], ID[:])
                mm.then_inc(made["T"], 1)

            def project(kind, i, m, p):
                ps = free_for(pe, kind, m)
                pe.wait_ge(xnT_ready, m + 1)
                pe.matmul(ps[:], Wq5[:, i, :], xnT[:], start=True, stop=True)\
                    .then_inc(made[kind], 1)

            def project_v(m, p):
                ps = free_for(pe, "v", m)
                for c in range(NC):
                    mm = pe.matmul(ps[:, c * P:(c + 1) * P], xnT[:, c * P:(c + 1) * P], Wv[:],
                                   start=True, stop=True)
                mm.then_inc(made["v"], 1)

            def front_kt(m, p):
                ps = free_for(pe, "kt", m)
                pe.wait_ge(qk_ready, 2 * m + 2)
                for c in range(NC):
                    mm = pe.transpose(ps[:, c * P:(c + 1) * P], kT[p][:, c * P:(c + 1) * P], ID[:])
                mm.then_inc(made["kt"], 1)

            def scores(n, p, s):
                c, hg = divmod(s, HG)
                if c == 0:
                    pe.wait_ge(qe_act, 8 * n + 2 * hg + 2)
                    pe.wait_ge(qe_pool, 4 * n + hg + 1)
                    pe.wait_ge(qe_dve, 4 * n + hg + 1)
                k = 16 * n + s
                if not (isinstance(k, int) and k < 4):
                    pe.wait_ge(p_ready, k - 3)
                cs = slice(c * P, (c + 1) * P)
                pe.matmul(bank[s % 4][:], kT[p][:, cs], QE[p][:, 4 * hg:4 * hg + 4, cs],
                          start=True, stop=True).then_inc(sc_ready, 1)

            def state(n, p, c):
                pe.wait_ge(ktok_ready, n + 1)
                k = 3 * n + c
                if not (isinstance(k, int) and k == 0):
                    pe.wait_ge(st_sb, k)
                pe.matmul(bank[5][:, 0:C], ktok[p][:, c, :], V[p][:, c, :], start=(c == 0),
                          stop=(c == 2), skip_group_check=True).then_inc(st_ready, 1)

            def mix_v(n, p, c):
                cs = slice(c * P, (c + 1) * P)
                if c == 0 and not (isinstance(n, int) and n == 0):
                    pe.wait_ge(y_sb, n)
                if c:
                    pe.wait_ge(st_sb, 3 * n + c)
                    pe.matmul(bank[4][:, cs], STsb[:, c, :], qT[p][:, cs], start=True, stop=False,
                              skip_group_check=True)
                pe.wait_ge(p_ready, 16 * n + 4 * c + 4)
                for i in range(HG):
                    for hg in range(HG):
                        mm = pe.matmul(bank[4][32 * hg:32 * hg + 32, cs],
                                       VE[p][:, c, i, 32 * hg:32 * hg + 32],
                                       PR[:, (4 * c + hg) % 8, i, :],
                                       start=(c == 0 and i == 0), stop=(i == HG - 1),
                                       skip_group_check=True)
                mm.then_inc(pv_done, 1)

            def group_mean(m):
                pe.wait_ge(gm_ready, m + 1)
                ps = free_for(pe, "gn", m)
                pe.matmul(ps[:, 0:2], HMEAN[:], gmv[:], start=True, stop=True).then_inc(made["gn"], 1)

            def project_out(m):
                pe.wait_ge(og_ready, m + 1)
                ps = free_for(pe, "proj", m)
                for c in range(NC):
                    mm = pe.matmul(ps[:, c * P:(c + 1) * P], og[:, c * P:(c + 1) * P], Wp[:],
                                   start=True, stop=True)
                mm.then_inc(made["proj"], 1)

            def step(n, p, front=True, tail=True):
                q = 1 - p
                for s in range(16):
                    scores(n, p, s)
                    if s == 0:
                        state(n, p, 0)
                    if s == 1 and tail:
                        mix_v(n - 1, q, 3)
                    if s == 2:
                        state(n, p, 1)
                    if s == 3 and tail:
                        group_mean(n - 1)
                    if s == 4:
                        state(n, p, 2)
                        if front:
                            front_T(n + 1, q)
                    if s == 5:
                        mix_v(n, p, 0)
                    if s == 9:
                        mix_v(n, p, 1)
                    if s == 13:
                        mix_v(n, p, 2)
                    if s == 8 and tail:
                        project_out(n - 1)
                    if front:
                        for at, kind, i in ((7, "q", 0), (9, "qs", 1), (10, "k", 2), (11, "ks", 3),
                                            (13, "g", 4)):
                            if s == at:
                                project(kind, i, n + 1, q)
                        if s == 12:
                            project_v(n + 1, q)
                        if s == 14:
                            front_kt(n + 1, q)

            pe.wait_ge(att_in, 16 * ATT_LOADS)
            front_T(0, 0)
            for kind, i in (("q", 0), ("qs", 1), ("k", 2), ("ks", 3)):
                project(kind, i, 0, 0)
            project_v(0, 0)
            project("g", 4, 0, 0)
            front_kt(0, 0)
            pe.wait_ge(ve_zero, 2)
            pe.wait_ge(v_ready, 5)
            steps(pe, None, lambda: step(0, 0, tail=False), step, lambda: step(B - 1, 1, front=False), 0)
            mix_v(B - 1, 1, 3)
            group_mean(B - 1)
            project_out(B - 1)

            def mixture(s):
                def tile_T(m):
                    pe.wait_ge(s["xn"], m + 1)
                    if not (isinstance(m, int) and m == 0):
                        pe.wait_ge(s["lr"], m)
                    for c in range(NC):
                        mm = pe.transpose(bank[6][:, c * P:(c + 1) * P], xn[:, c, :], ID[:])
                    mm.then_inc(s["T"], 1)

                def logits(m):
                    pe.wait_ge(s["xT"], m + 1)
                    for c in range(NC):
                        mm = pe.matmul(bank[6][:, c * E:(c + 1) * E], xnT[:, c * P:(c + 1) * P],
                                       RW[:], start=True, stop=True)
                    mm.then_inc(s["lg"], 1)

                def split_product(ps, w, cols, v, start, stop):
                    for a, (i, j) in enumerate(((0, 0), (0, 1), (1, 0))):
                        mm = pe.matmul(ps[:], w[i][cols], v[j][:], start=(start and a == 0),
                                       stop=(stop and a == 2))
                    return mm

                def up(n, p, k):
                    e, m = divmod(k, FC)
                    cols = (slice(None), e, slice(m * P, (m + 1) * P))
                    i = NCH * n + k
                    early = isinstance(i, int) and i < 2
                    if not early:
                        pe.wait_ge(s["sa"], i - 1)
                    split_product(bank[k % 2], W1, cols, xs[p], True, True).then_inc(s["a"], 1)
                    if not early:
                        pe.wait_ge(s["h"], i - 1)
                    split_product(bank[2 + k % 2], W3, cols, xs[p], True, True).then_inc(s["b"], 1)

                def down(n, k):
                    e, m = divmod(k, FC)
                    i = NCH * n + k
                    if m == 0:
                        o = 4 * n + e
                        if not (isinstance(o, int) and o < 2):
                            pe.wait_ge(s["o"], o - 1)
                    pe.wait_ge(s["lo"], i + 1)
                    mm = split_product(bank[4 + e % 2], W2, (slice(None), k, slice(None)), hs[k % 4],
                                       m == 0, m == FC - 1)
                    if m == FC - 1:
                        mm.then_inc(s["tr"], 1)

                def tile_back(m):
                    pe.wait_ge(s["od"], m + 1)
                    for c in range(NC):
                        mm = pe.transpose(bank[7][:, c * P:(c + 1) * P],
                                          oacc[0][:, c * P:(c + 1) * P], ID[:])
                    mm.then_inc(s["pr"], 1)

                def step(n, p, front=True, tail=True):
                    pe.wait_ge(s["xs"], 2 * n + 2)
                    for k in range(NCH):
                        up(n, p, k)
                        if k >= 2:
                            down(n, k - 2)
                        elif tail:
                            down(n - 1, NCH - 2 + k)
                        if k == 4 and tail:
                            tile_back(n - 1)
                        if k == 6 and front:
                            tile_T(n + 1)
                        if k == 10 and front:
                            logits(n + 1)

                tile_T(0)
                logits(0)
                if s is mix[0]:
                    pe.wait_ge(w13_lo, 2)
                    pe.wait_ge(w2_lo, 1)
                steps(pe, None, lambda: step(0, 0, tail=False), step,
                      lambda: step(B - 1, 1, front=False), 0)
                down(B - 1, NCH - 2)
                down(B - 1, NCH - 1)
                tile_back(B - 1)

            def s4d():
                def turn(b):
                    pe.wait_ge(s_xn, b + 1)
                    if b >= 2:
                        pe.wait_ge(s_xT, b - 1)
                    for c in range(NC):
                        mm = pe.transpose(bank[6 + b % 2][:, c * P:(c + 1) * P], xns[b % 2][:, c, :], ID[:])
                    mm.then_inc(s_T, 1)

                turn(0)
                turn(1)
                pe.wait_ge(dk_ready, 1)
                for b in range(B):
                    pe.wait_ge(s_xT, b + 1)
                    if b >= 2:
                        pe.wait_ge(x3_done, b - 1)
                    for c in range(NC):
                        cs = slice(c * P, (c + 1) * P)
                        for l in range(b + 1):
                            mm = pe.matmul(bank[b % 2][:, cs], XT[:, b - l, cs], DK[:, l, :],
                                           start=(l == 0), stop=(l == b))
                    mm.then_inc(s_y, 1)
                    if b + 2 < B:
                        turn(b + 2)

            if stop >= 2:
                pe.wait_ge(x1_done, B)
                mixture(mix[0])
            if stop >= 3:
                pe.wait_ge(mix[0]["xd"], B)
                s4d()
            if stop >= 4:
                pe.wait_ge(x3_done, 8)
                mixture(mix[1])

        @block.scalar
        def _(act):
            def spread(m, p, k):
                hg, i = divmod(k, 2)
                h = 4 * hg + 3 * i
                if k == 0:
                    act.wait_ge(qk_ready, 2 * m + 1)
                nc.scalar.activation(QE[p][:, h, :], qT[p][:], ACT.Copy,
                                     scale=ONEHOT[:, h:h + 1]).then_inc(qe_act, 1)

            def front(m, p):
                ps = ready_for(act, "T", m)
                nc.scalar.activation(xnT[:], ps[:], ACT.Copy).then_inc(xnT_ready, 1)
                for k in range(4):
                    spread(m, p, k)
                ps = ready_for(act, "v", m)
                nc.scalar.activation(V[p][:].rearrange("p c h -> p (c h)"), ps[:], ACT.Copy)\
                    .then_inc(v_ready, 1)
                pv = ps[:].rearrange("p (c g i d) -> p c g i d", c=NC, g=HG, i=HG)
                vv = VE[p][:].rearrange("p c i (g j d) -> p c i g j d", g=HG, j=HG)
                for i in range(HG):
                    nc.scalar.activation(vv[:, :, i, :, i, :], pv[:, :, :, i, :], ACT.Copy)\
                        .then_inc(v_ready, 1)
                ps = ready_for(act, "g", m)
                nc.scalar.activation(SG[p][:], ps[:], ACT.Silu).then_inc(sg_ready, 1)
                for k in range(4, 8):
                    spread(m, p, k)
                ps = ready_for(act, "kt", m)
                nc.scalar.activation(ktok[p][:].rearrange("p c h -> p (c h)"), ps[:], ACT.Copy)\
                    .then_inc(ktok_ready, 1)

            def read_y(m):
                act.wait_ge(pv_done, 4 * m + 4)
                nc.scalar.activation(Ysb[:], bank[4][:], ACT.Copy).then_inc(y_sb, 1)

            def step(n, p):
                read_y(n - 1)
                front(n + 1, 1 - p)

            def first():
                act.wait_ge(ve_zero, 2)
                front(0, 0)
                act.wait_ge(w13_in, 32)
                nc.scalar.activation(W1[0][:], W1raw, ACT.Copy).then_inc(w13_hi, 1)
                nc.scalar.activation(W3[0][:], W3raw, ACT.Copy).then_inc(w13_hi, 1)
                act.wait_ge(w13_lo, 2)
                front(1, 1)

            act.wait_ge(att_in, 16 * ATT_LOADS)
            steps(act, None, first, step, lambda: read_y(B - 2), 0)
            read_y(B - 1)

            def mixture(s):
                def front(m):
                    act.wait_ge(s["T"], m + 1)
                    if not (isinstance(m, int) and m == 0):
                        act.wait_ge(s["xs"], 2 * m)
                        act.wait_ge(s["lg"], m)
                    nc.scalar.activation(xnT[:], bank[6][:], ACT.Copy).then_inc(s["xT"], 1)

                def high(i, k):
                    act.wait_ge(s["h"], i + 1)
                    nc.scalar.activation(hs[k % 4][0][:], hf[k % 2][:], ACT.Copy).then_inc(s["hi"], 1)

                def step(n, p, front_=True):
                    for k in range(NCH):
                        i = NCH * n + k
                        act.wait_ge(s["a"], i + 1)
                        if not (isinstance(i, int) and i < 2):
                            act.wait_ge(s["h"], i - 1)
                        nc.scalar.activation(sa[k % 2][:], bank[k % 2][:], ACT.Silu)\
                            .then_inc(s["sa"], 1)
                        if not (isinstance(i, int) and i < 1):
                            high(i - 1, (k - 1) % NCH)
                        if k == 7 and front_:
                            front(n + 1)

                front(0)
                steps(act, None, lambda: step(0, 0), step, lambda: step(B - 1, 1, False), 0)
                high(NCH * B - 1, NCH - 1)

            if stop >= 2:
                act.wait_ge(x1_done, B)
                act.wait_ge(w2_in, 16)
                nc.scalar.activation(W2[0][:], GB[1][:].rearrange("p t e -> p (t e)")
                                     .rearrange("p (k c) -> p k c", c=C), ACT.Copy).then_inc(w2_hi, 1)
                mixture(mix[0])
            if stop >= 3:
                for b in range(B):
                    act.wait_ge(s_T, b + 1)
                    nc.scalar.activation(XT[:, b, :], bank[6 + b % 2][:], ACT.Copy).then_inc(s_xT, 1)
            if stop >= 4:
                mixture(mix[1])

        @block.vector
        def _(dve):
            own = Own(dve, dve_own)
            tt, ts, stt = nc.vector.tensor_tensor, nc.vector.tensor_scalar, nc.vector.scalar_tensor_tensor

            def norm_stats(src, ready):
                for c in range(NC):
                    own.did(nc.vector.bn_stats(stats[:, c, :], src[c]))
                wait_apart(dve, dve_own, own.base + own.k)
                for c in range(NC):
                    own.did(nc.vector.bn_aggr(mv[:, c, :], stats[:, c, :]))
                own.wait()
                ts(veps[:], mv[:, :, 1], EPS, None, ALU.add).then_inc(ready, 1)

            def norm_apply(src, done):
                for c in range(NC):
                    a = ts(xn[:, c, :], src[c], mv[:, c, 0:1], rstd[:, c:c + 1], ALU.subtract, ALU.mult)
                a.then_inc(done, 1)

            def tiles(m):
                xb = X[:, bass.ds(m, 1)] if not isinstance(m, int) else X[:, m:m + 1]
                return [xb[:, 0, c, :] for c in range(NC)]

            def a_stats(m):
                if isinstance(m, int):
                    dve.wait_ge(*[(x_first, 16), (x_second, 16), (x_rest, 16 * (B - 2))][min(m, 2)])
                norm_stats(tiles(m), a_ve)

            def a_apply(m):
                dve.wait_ge(a_rs, m + 1)
                if not (isinstance(m, int) and m == 0):
                    dve.wait_ge(made["T"], m)
                norm_apply(tiles(m), a_xn)

            def rope_half(m, p, kind, i, dst):
                ps = ready_for(dve, kind, m)
                if kind == "q" and not (isinstance(m, int) and m < 2):
                    dve.wait_ge(og_ready, m - 1)
                tt(dst[:], ps[:], RP[:, i, :], ALU.mult).then_inc(rope_done, 1)

            def rope_add(m, dst, i):
                dve.wait_ge(rope_done, 4 * m + 2 * i + 2)
                tt(dst[:], t1[:], t2[:], ALU.add).then_inc(qk_ready, 1)

            def spread(m, p, hg):
                h = 4 * hg + 2
                dve.wait_ge(qk_ready, 2 * m + 1)
                ts(QE[p][:, h, :], qT[p][:], ONEHOT[:, h:h + 1], None, ALU.mult).then_inc(qe_dve, 1)

            def mask(n, p, s):
                c, hg = divmod(s, HG)
                if hg == 0:
                    k = 4 * n + c
                    if not (isinstance(k, int) and k < 2):
                        dve.wait_ge(pv_done, k - 1)
                dve.wait_ge(sc_ready, 16 * n + s + 1)
                tt(PR[:, s % 8], bank[s % 4][:].rearrange("p (i t) -> p i t", i=HG), CAUS[:],
                   ALU.mult).then_inc(p_ready, 1)

            def state(n, p, c):
                dve.wait_ge(st_ready, 3 * n + c)
                if not (isinstance(n, int) and n == 0):
                    dve.wait_ge(pv_done, 4 * (n - 1) + c + 1)
                tt(STsb[:, c, :], bank[5][:, 0:C], SAME[:], ALU.mult).then_inc(st_sb, 1)

            def group_a(m):
                dve.wait_ge(y_sb, m + 1)
                own.did(nc.vector.bn_stats(gs6[:], Ysb[:]))
                wait_apart(dve, dve_own, own.base + own.k)
                own.link(nc.vector.bn_aggr(gmv[:], gs6[:]))
                stt(out=gmv[:, 1:2], in0=gmv[:, 0:1], scalar=gmv[:, 0:1], in1=gmv[:, 1:2],
                    op0=ALU.mult, op1=ALU.add).then_inc(gm_ready, 1)

            def group_b(m):
                ps = ready_for(dve, "gn", m)
                nc.vector.tensor_copy(gst[:], ps[:, 0:2]).then_inc(gn_read, 1)
                dve.wait_ge(gn_read, m + 1)
                own.link(stt(out=gsm[:, 0:1], in0=gst[:, 0:1], scalar=gst[:, 0:1], in1=gst[:, 1:2],
                             op0=ALU.mult, op1=ALU.subtract))
                ts(gsm[:, 1:2], gsm[:, 0:1], -1.0, EPS, ALU.mult, ALU.add).then_inc(gv_ready, 1)

            def group_c(m, p):
                dve.wait_ge(gr_ready, m + 1)
                own.link(tt(gsm[:, 3:4], gsm[:, 2:3], GN[:, 0:1], ALU.mult))
                own.link(stt(out=gsm[:, 4:5], in0=gst[:, 0:1], scalar=gsm[:, 3:4], in1=GN[:, 1:2],
                             op0=ALU.mult, op1=ALU.subtract))
                dve.wait_ge(sg_ready, m + 1)
                own.link(ts(t1[:], Ysb[:], gsm[:, 3:4], gsm[:, 4:5], ALU.mult, ALU.subtract))
                tt(og[:], t1[:], SG[p][:], ALU.mult).then_inc(og_ready, 1)

            def residual(m):
                ps = ready_for(dve, "proj", m)
                xb = X[:, bass.ds(m, 1)] if not isinstance(m, int) else X[:, m:m + 1]
                xb = xb.rearrange("p o c h -> p (o c h)")
                tt(xb, ps[:], xb, ALU.add).then_inc(x1_done, 1)

            def step(n, p, front=True, tail=True):
                q = 1 - p
                for s in range(16):
                    mask(n, p, s)
                    if s == 0 and front:
                        a_stats(n + 1)
                    if s in (1, 3, 5):
                        state(n, p, s // 2 + 1)
                    if s == 2 and tail:
                        group_a(n - 1)
                    if s == 3 and front:
                        a_apply(n + 1)
                    if s == 4 and tail:
                        group_b(n - 1)
                    if s == 6 and tail:
                        group_c(n - 1, q)
                    if s == 8 and tail:
                        residual(n - 1)
                    if front:
                        if s == 7:
                            rope_half(n + 1, q, "q", 0, t1)
                        if s == 9:
                            rope_half(n + 1, q, "qs", 1, t2)
                            rope_add(n + 1, qT[q], 0)
                        if s == 10:
                            dve.wait_ge(qk_ready, 2 * (n + 1) + 1)
                            rope_half(n + 1, q, "k", 2, t1)
                        if s == 11:
                            rope_half(n + 1, q, "ks", 3, t2)
                            rope_add(n + 1, kT[q], 1)
                        if s >= 12:
                            spread(n + 1, q, s - 12)

            def first():
                a_stats(0)
                a_apply(0)
                rope_half(0, 0, "q", 0, t1)
                rope_half(0, 0, "qs", 1, t2)
                rope_add(0, qT[0], 0)
                dve.wait_ge(qk_ready, 1)
                rope_half(0, 0, "k", 2, t1)
                rope_half(0, 0, "ks", 3, t2)
                rope_add(0, kT[0], 1)
                for hg in range(HG):
                    spread(0, 0, hg)
                dve.wait_ge(w13_lo, 2)
                step(0, 0, tail=False)

            nc.vector.memset(half[:], -0.5).then_inc(const_set, 1)
            dve.wait_ge(att_in, 16 * ATT_LOADS)
            steps(dve, own, lambda: (first(), dve.wait_ge(x_rest, 16 * (B - 2))), step,
                  lambda: step(B - 1, 1, front=False), 8 + 2 + 1 + 3)
            group_a(B - 1)
            group_b(B - 1)
            group_c(B - 1, 1)
            residual(B - 1)

            def mixture(s, before):
                def m_stats(m):
                    norm_stats(tiles(m), s["ve"])

                def m_apply(m):
                    dve.wait_ge(s["rs"], m + 1)
                    if not (isinstance(m, int) and m == 0):
                        dve.wait_ge(s["T"], m)
                    norm_apply(tiles(m), s["xn"])

                def split_x(m, p):
                    dve.wait_ge(s["xT"], m + 1)
                    if not (isinstance(m, int) and m < 2):
                        dve.wait_ge(s["b"], NCH * (m - 1))
                    nc.vector.tensor_copy(xs[p][0][:], xnT[:]).then_inc(s["xs"], 1)
                    dve.wait_ge(s["xs"], 2 * m + 1)
                    tt(xs[p][1][:], xnT[:], xs[p][0][:].bitcast(F32), ALU.subtract)\
                        .then_inc(s["xs"], 1)

                def route_a(m):
                    dve.wait_ge(s["lg"], m + 1)
                    tt(LG[:], bank[6][:, 0:NC * E].rearrange("p (c e) -> p c e", e=E),
                           RB[:].to_broadcast([P, NC, E]), ALU.add).then_inc(s["lr"], 1)
                    dve.wait_ge(s["lr"], m + 1)
                    own.link(nc.vector.tensor_reduce(mx[:], LG[:], AX_X, ALU.max))
                    tt(LD[:], LG[:], mx[:].unsqueeze(2).to_broadcast([P, NC, E]), ALU.subtract)\
                        .then_inc(s["pr_in"], 1)

                def route_b(m):
                    lj = LG[:].unsqueeze(2).to_broadcast([P, NC, E, E])
                    li = LG[:].unsqueeze(3).to_broadcast([P, NC, E, E])
                    own.did(tt(GT[:], lj, li, ALU.is_gt))
                    own.link(tt(EQ[:], lj, li, ALU.is_equal))
                    own.link(tt(EQ[:], EQ[:], LOWER[:], ALU.mult))
                    own.link(tt(GT[:], GT[:], EQ[:], ALU.add))
                    own.link(nc.vector.tensor_reduce(rank[:], GT[:], AX_X, ALU.add))
                    own.link(ts(rank[:], rank[:], 1.5, None, ALU.is_lt))
                    dve.wait_ge(s["le"], m + 1)
                    own.link(tt(pm[:], LE[:], rank[:], ALU.mult))
                    own.link(nc.vector.tensor_reduce(smr[:], pm[:], AX_X, ALU.add))
                    own.link(nc.vector.reciprocal(smr[:], smr[:]))
                    if not (isinstance(m, int) and m == 0):
                        dve.wait_ge(s["gst"], 16 * m)
                    tt(G[:], pm[:], smr[:].unsqueeze(2).to_broadcast([P, NC, E]), ALU.mult)\
                        .then_inc(s["gates"], 1)

                def hidden(i, k):
                    dve.wait_ge(s["sa"], i + 1)
                    dve.wait_ge(s["b"], i + 1)
                    if not (isinstance(i, int) and i < 2):
                        dve.wait_ge(s["lo"], i - 1)
                    tt(hf[k % 2][:], bank[2 + k % 2][:], sa[k % 2][:], ALU.mult).then_inc(s["h"], 1)

                def low(i, k):
                    dve.wait_ge(s["hi"], i + 1)
                    tt(hs[k % 4][1][:], hf[k % 2][:], hs[k % 4][0][:].bitcast(F32), ALU.subtract)\
                        .then_inc(s["lo"], 1)

                def gated(n, p, e):
                    if e == 0:
                        dve.wait_ge(s["gld"], 16 * (n + 1))
                        if not (isinstance(n, int) and n == 0):
                            dve.wait_ge(s["pr"], n)
                    o = 4 * n + e
                    dve.wait_ge(s["tr"], o + 1)
                    dst = oacc[0] if e == 0 else otmp
                    tt(dst[:], bank[4 + e % 2][:], GB[p][:, :, e], ALU.mult).then_inc(s["o"], 1)
                    dve.wait_ge(s["o"], o + 1)
                    if e:
                        a = tt(oacc[0][:], oacc[0][:], otmp[:], ALU.add)
                        if e == E - 1:
                            a.then_inc(s["od"], 1)
                        else:
                            own.did(a)

                def residual(m):
                    dve.wait_ge(s["pr"], m + 1)
                    xb = X[:, bass.ds(m, 1)] if not isinstance(m, int) else X[:, m:m + 1]
                    xb = xb.rearrange("p o c h -> p (o c h)")
                    tt(xb, bank[7][:], xb, ALU.add).then_inc(s["xd"], 1)

                def step(n, p, front=True, tail=True):
                    q = 1 - p
                    for k in range(NCH):
                        i = NCH * n + k
                        hidden(i, k)
                        if not (isinstance(i, int) and i < 1):
                            low(i - 1, (k - 1) % NCH)
                        if k in (6, 10, 14):
                            gated(n, p, k // 4 - 1)
                        if tail and k == 2:
                            gated(n - 1, q, 3)
                        if tail and k == 5:
                            residual(n - 1)
                        if front:
                            if k == 1:
                                m_stats(n + 1)
                            if k == 4:
                                m_apply(n + 1)
                            if k == 8:
                                split_x(n + 1, q)
                            if k == 11:
                                route_a(n + 1)
                            if k == 13:
                                route_b(n + 1)

                def first():
                    m_stats(0)
                    m_apply(0)
                    split_x(0, 0)
                    route_a(0)
                    route_b(0)
                    before()
                    step(0, 0, tail=False)

                steps(dve, own, first, step, lambda: step(B - 1, 1, front=False), 8 + 1 + 9 + 2)
                low(NCH * B - 1, NCH - 1)
                gated(B - 1, 1, 3)
                residual(B - 1)

            def split_w2():
                dve.wait_ge(w2_hi, 1)
                tt(W2[1][:], GB[1][:].rearrange("p t e -> p (t e)").rearrange("p (k c) -> p k c", c=C),
                   W2[0][:].bitcast(F32), ALU.subtract).then_inc(w2_lo, 1)

            def s4d():
                def s_stats(b):
                    i = b % 2
                    for c in range(NC):
                        own.did(nc.vector.bn_stats(sst[:, i, c, :], X[:, b, c, :]))
                    own.wait()
                    for c in range(NC):
                        own.did(nc.vector.bn_aggr(smv[:, i, c, :], sst[:, i, c, :]))
                    own.wait()
                    ts(sve[:, i, :], smv[:, i, :, 1], EPS, None, ALU.add).then_inc(s_ve, 1)

                def s_apply(b):
                    i = b % 2
                    dve.wait_ge(s_rs, b + 1)
                    if b >= 2:
                        dve.wait_ge(s_T, b - 1)
                    for c in range(NC):
                        a = ts(xns[i][:, c, :], X[:, b, c, :], smv[:, i, c, 0:1], srs[:, i, c:c + 1],
                               ALU.subtract, ALU.mult)
                    a.then_inc(s_xn, 1)

                s_stats(0)
                s_stats(1)
                s_apply(0)
                dve.wait_ge(k_ready, 1)
                for l in range(B):
                    a = ts(DK[:, l, :], ID[:], K[:, l:l + 1], None, ALU.mult)
                a.then_inc(dk_ready, 1)
                s_apply(1)
                for b in range(B):
                    if b + 2 < B:
                        s_stats(b + 2)
                        s_apply(b + 2)
                    dve.wait_ge(s_y, b + 1)
                    xb = X[:, b].rearrange("p c h -> p (c h)")
                    tt(xb, bank[b % 2][:], xb, ALU.add).then_inc(x3_done, 1)

            if stop >= 2:
                dve.wait_ge(x1_done, B)
                dve.wait_ge(ffn_in, 16 * FFN_LOADS)
                mixture(mix[0], split_w2)
            if stop >= 3:
                dve.wait_ge(mix[0]["xd"], B)
                dve.wait_ge(par_in, 16 * PAR_LOADS)
                s4d()
            if stop >= 4:
                dve.wait_ge(x3_done, 8)
                mixture(mix[1], lambda: None)

        @block.gpsimd
        def _(pool):
            own = Own(pool, pool_own)
            tt, ts = nc.gpsimd.tensor_tensor, nc.gpsimd.tensor_scalar

            def spread(m, p, hg):
                h = 4 * hg + 1
                if hg == 0:
                    wait_apart(pool, qk_ready, 2 * m + 1)
                ts(QE[p][:, h, :], qT[p][:], ONEHOT[:, h:h + 1], None, ALU.mult).then_inc(qe_pool, 1)

            def inverse_root(ready, k, out_, in_, n, done):
                pool.wait_ge(ready, k + 1)
                tt(out_, in_, half[:, 0:n], ALU.pow).then_inc(done, 1)

            def step(n, p):
                inverse_root(a_ve, n + 1, rstd[:], veps[:], NC, a_rs)
                inverse_root(gv_ready, n - 1, gsm[:, 2:3], gsm[:, 1:2], 1, gr_ready)
                for hg in range(HG):
                    spread(n + 1, 1 - p, hg)

            def first():
                inverse_root(a_ve, 0, rstd[:], veps[:], NC, a_rs)
                for hg in range(HG):
                    spread(0, 0, hg)
                for i, (W, raw) in enumerate(((W1, W1raw), (W3, W3raw))):
                    pool.wait_ge(w13_hi, i + 1)
                    tt(W[1][:], raw, W[0][:].bitcast(F32), ALU.subtract).then_inc(w13_lo, 1)
                inverse_root(a_ve, 1, rstd[:], veps[:], NC, a_rs)
                for hg in range(HG):
                    spread(1, 1, hg)

            pool.wait_ge(const_set, 1)
            for v in VE:
                nc.gpsimd.memset(v[:], 0.0).then_inc(ve_zero, 1)
            pool.wait_ge(att_in, 16 * ATT_LOADS)
            steps(pool, None, first, step,
                  lambda: inverse_root(gv_ready, B - 2, gsm[:, 2:3], gsm[:, 1:2], 1, gr_ready), 0)
            inverse_root(gv_ready, B - 1, gsm[:, 2:3], gsm[:, 1:2], 1, gr_ready)

            def kernel_terms():
                pool.wait_ge(par_in, 16 * PAR_LOADS)

                def row(i):
                    return rows[:, i, :]

                free = [2]

                def new():
                    free[0] += 1
                    return row(free[0] - 1)

                def mul(a, b, o=None):
                    o = new() if o is None else o
                    own.link(tt(o, a, b, ALU.mult))
                    return o

                def add(a, b, op=ALU.add, o=None):
                    o = new() if o is None else o
                    own.link(tt(o, a, b, op))
                    return o

                def lin(a, m, c):
                    o = new()
                    own.link(ts(o, a, m, c, ALU.mult, ALU.add))
                    return o

                def exp(a):
                    o = new()
                    own.link(tt(o, EULER[:], a, ALU.pow))
                    return o

                ld = new()
                own.link(nc.gpsimd.tensor_copy(ld, DT[:].to_broadcast([P, NS])))
                dt_ = exp(ld)
                zr = lin(mul(dt_, exp(row(0))), -0.5, 0.0)
                zi = lin(mul(dt_, row(1)), 0.5, 0.0)
                one = lin(zr, -1.0, 1.0)
                zi2 = mul(zi, zi)
                den = add(mul(one, one), zi2)
                ones = lin(zr, 0.0, -1.0)
                iden = new()
                own.link(tt(iden, den, ones, ALU.pow))
                ar = mul(add(lin(mul(zr, zr), -1.0, 1.0), zi2, ALU.subtract), iden)
                ai = mul(lin(zi, 2.0, 0.0), iden)
                br, bi, cr, ci = (BC4[:, i] for i in range(4))
                pr_ = add(mul(br, cr), mul(bi, ci), ALU.subtract)
                pi_ = add(mul(br, ci), mul(bi, cr))
                w = lin(mul(dt_, iden), 0.5, 0.0)
                er, ei = mul(w, one), mul(w, zi)
                add(mul(pr_, er), mul(pi_, ei), ALU.subtract, L2[:, 0, 0, :])
                add(mul(pr_, ei), mul(pi_, er), ALU.add, L2[:, 0, 1, :])
                re, im = ar, ai
                for k in range(3):
                    n = 1 << k
                    low, high = L2[:, 0:n], L2[:, n:2 * n]
                    rv, iv = (v.unsqueeze(1).to_broadcast([P, n, NS]) for v in (re, im))
                    t0, t1_ = tmp[:, 0:n, 0, :], tmp[:, 0:n, 1, :]
                    own.did(tt(t0, low[:, :, 1, :], iv, ALU.mult))
                    own.did(tt(t1_, low[:, :, 1, :], rv, ALU.mult))
                    own.did(tt(high[:, :, 0, :], low[:, :, 0, :], rv, ALU.mult))
                    own.link(tt(high[:, :, 1, :], low[:, :, 0, :], iv, ALU.mult))
                    own.did(tt(high[:, :, 0, :], high[:, :, 0, :], t0, ALU.subtract))
                    own.link(tt(high[:, :, 1, :], high[:, :, 1, :], t1_, ALU.add))
                    if k < 2:
                        re, im = (add(mul(re, re), mul(im, im), ALU.subtract),
                                  lin(mul(re, im), 2.0, 0.0))
                w = NS // 2
                while w:
                    own.link(tt(L2[:, :, 0, 0:w], L2[:, :, 0, 0:w], L2[:, :, 0, w:2 * w], ALU.add))
                    w //= 2
                own.did(tt(K[:, 0:1], L2[:, 0, 0, 0:1], DD[:], ALU.add))
                nc.gpsimd.tensor_copy(K[:, 1:B], L2[:, 1:B, 0, 0]).then_inc(k_ready, 1)

            def mixture(s):
                def front(m):
                    inverse_root(s["ve"], m, rstd[:], veps[:], NC, s["rs"])
                    pool.wait_ge(s["pr_in"], m + 1)
                    e16 = EULER[:, 0:NC * E].rearrange("p (c e) -> p c e", e=E)
                    tt(LE[:], e16, LD[:], ALU.pow).then_inc(s["le"], 1)

                def step(n, p):
                    front(n + 1)

                front(0)
                steps(pool, None, lambda: step(0, 0), step, lambda: None, 0)

            if stop >= 2:
                pool.wait_ge(x1_done, B)
                own.link(nc.gpsimd.memset(EULER[:], float(np.e)))
                mixture(mix[0])
            if stop >= 3:
                kernel_terms()
                for b in range(B):
                    inverse_root(s_ve, b, srs[:, b % 2, :], sve[:, b % 2, :], NC, s_rs)
            if stop >= 4:
                mixture(mix[1])


def launch_arrays(inputs):
    def f(name):
        return np.ascontiguousarray(inputs[name])

    w = f("L0_attn_a_w_qkv")
    swap = np.arange(C) ^ 1
    q, k, v = w[0:C], w[C:2 * C], w[2 * C:]
    w5 = np.stack([q.T, q[swap].T, k.T, k[swap].T, f("L0_attn_a_w_gated").T], axis=1)
    arrays = {
        "x": f("L0_attn_a_x"), "w5": w5, "wv": v.T, "wp": f("L0_attn_a_w_proj").T,
        "gn": np.stack([f("L0_attn_a_gn_weight"), f("L0_attn_a_gn_bias")], axis=1),
        "log_dt": f("L0_attn_b_log_dt"), "log_a": f("L0_attn_b_log_A_real"), "a_im": f("L0_attn_b_A_imag"),
        "bc": f("L0_attn_b_B").transpose(0, 2, 1), "cc": f("L0_attn_b_C").transpose(0, 2, 1), "dd": f("L0_attn_b_D"),
        "rw": f("L0_ffn_router_w"), "rb": f("L0_ffn_router_b"),
        "w1": f("L0_ffn_w1"), "w3": f("L0_ffn_w3"), "w2": f("L0_ffn_w2"),
    }
    arrays |= constants()
    return {n: np.ascontiguousarray(a) for n, a in arrays.items()}


def kernel(**inputs):
    import concourse.bacc as bacc
    from concourse.bass_utils import run_bass_kernel_spmd

    nc = bacc.Bacc("TRN2", target_bir_lowering=False, num_devices=1)
    arrays = launch_arrays(inputs)
    args = [nc.dram_tensor(n, a.shape, mybir.dt.from_np(a.dtype), kind="ExternalInput").ap()
            for n, a in arrays.items()]
    out = nc.dram_tensor("out", (B, T, C), F32, kind="ExternalOutput").ap()
    build(nc, *args, out)
    return run_bass_kernel_spmd(nc, [arrays], core_ids=[0]).results[0]["out"]
```

```python
from contextlib import ExitStack

import numpy as np

import concourse.bass as bass
from concourse import mybir

F32 = mybir.dt.float32
F32R = mybir.dt.float32r
ALU = mybir.AluOpType
ACT = mybir.ActivationFunctionType
AX_X = mybir.AxisListType.X

P = 128
B, T, C = 8, 512, 128
NC = T // P
H, HD = 16, 8
HG = 4
E, F = 4, 512
FC = F // P
NCH = E * FC
NS = 16
EPS = 1e-5
PER_TURN = (28, 40, 40)
BEHIND = 3
LATE, PARTS = 16 * 5, 16 * 6


def constants():
    d = np.arange(0, HD, 2, dtype=np.float64)
    inv_freq = 1.0 / 10000.0 ** (d / HD)
    t = np.arange(T, dtype=np.float64)
    scale = ((d + 0.4 * HD) / (1.4 * HD))[:, None] ** ((t - T // 2) / 512.0)[None, :]
    cos, sin = np.cos(inv_freq[:, None] * t), np.sin(inv_freq[:, None] * t)
    gamma = 1.0 - 2.0 ** (-5.0 - np.arange(H, dtype=np.float64))
    rope = np.zeros((C, 4, T))
    for c in range(C):
        h, i, odd = c // HD, c % HD // 2, c % 2
        sign = 1.0 if odd else -1.0
        up, down = gamma[h] ** t * HD ** -0.5, gamma[h] ** -t
        rope[c] = (cos[i] * scale[i] * up, sign * sin[i] * scale[i] * up,
                   cos[i] / scale[i] * down, sign * sin[i] / scale[i] * down)
    i = np.arange(P)
    head = i // HD
    same = (head[:, None] == head[None, :]).astype(np.float64)
    causal = np.broadcast_to((i[:, None] <= i[None, :]).astype(np.float64)[:, None, :], (P, HG, P))
    onehot = (head[:, None] == np.arange(H)[None, :]).astype(np.float64)
    lower = np.broadcast_to(np.tril(np.ones((E, E)), -1), (P, NC, E, E))
    tables = {
        "rope": rope, "causal": causal, "same_head": same, "head_mean": same / HD,
        "onehot": onehot, "ident": np.eye(P), "lower": lower,
    }
    return {n: np.ascontiguousarray(a, dtype=np.float32) for n, a in tables.items()}


class Own:

    def __init__(self, eng, sem):
        self.eng, self.sem, self.base, self.k, self.loops = eng, sem, 0, 0, 0

    def did(self, ins):
        ins.then_inc(self.sem, 1)
        self.k += 1

    def link(self, ins):
        self.did(ins)
        self.wait()

    def wait(self, back=0):
        self.eng.wait_ge(self.sem, self.base + self.k - back)


def steps(eng, own, first, step, last):
    first()
    if own is None:
        with eng.Fori(0, (B - 2) // 2) as j:
            step(2 * j + 1, 1)
            step(2 * j + 2, 0)
    else:
        k0, per = own.k, PER_TURN[own.loops]
        with eng.Fori(0, (B - 2) // 2) as j:
            own.base, own.k = k0 + j * per, 0
            step(2 * j + 1, 1)
            step(2 * j + 2, 0)
            assert own.k == per, own.k
        own.base, own.k = 0, k0 + (B - 2) // 2 * per
        own.loops += 1
    last()


def build(nc, x, w5, wv, wp, gn, log_dt, log_a, a_im, bc, cc, dd, rw, rb, w1, w3, w2,
          rope, causal, same_head, head_mean, onehot, ident, lower, out):
    ctx = ExitStack()
    with ctx:
        def sem(name):
            return ctx.enter_context(nc.semaphore(name))

        def alloc(stack, name, shape, dt=F32):
            return stack.enter_context(nc.sbuf_tensor(name, shape, dt))

        bank = [ctx.enter_context(nc.psum_tensor(f"bank{i}", [P, 512], F32)) for i in range(8)]
        gate_rows = nc.dram_tensor("gate_rows", (2, 2, P * NC * E), F32, kind="Internal").ap()

        X = alloc(ctx, "X", [P, B, NC, C])
        W1 = [alloc(ctx, f"W1{s}", [P, E, F], F32R) for s in ("hi", "lo")]
        W3 = [alloc(ctx, f"W3{s}", [P, E, F], F32R) for s in ("hi", "lo")]
        ID = alloc(ctx, "ID", [P, P])
        stats = alloc(ctx, "stats", [P, NC, 6])
        mv = alloc(ctx, "mv", [P, NC, 2])
        veps = alloc(ctx, "veps", [P, NC])
        rstd = alloc(ctx, "rstd", [P, NC])
        half = alloc(ctx, "half", [P, 32])
        xn = alloc(ctx, "xn", [P, NC, C])
        xnT = alloc(ctx, "xnT", [P, T])
        RW = alloc(ctx, "RW", [P, P])
        RB = alloc(ctx, "RB", [P, 1, E])
        LG = alloc(ctx, "LG", [P, NC, E])
        LD = alloc(ctx, "LD", [P, NC, E])
        LE = alloc(ctx, "LE", [P, NC, E])
        mx = alloc(ctx, "mx", [P, NC])
        GT = alloc(ctx, "GT", [P, NC, E, E])
        EQ = alloc(ctx, "EQ", [P, NC, E, E])
        LOWER = alloc(ctx, "LOWER", [P, NC, E, E])
        rank = alloc(ctx, "rank", [P, NC, E])
        pm = alloc(ctx, "pm", [P, NC, E])
        smr = alloc(ctx, "smr", [P, NC])
        G = alloc(ctx, "G", [P, NC, E])
        EULER = alloc(ctx, "EULER", [P, NS])
        xs = [[alloc(ctx, f"x{s}0", [P, T], F32R) for s in ("hi", "lo")]]
        GB = [alloc(ctx, "GB0", [P, T, E])]

        att = ExitStack()
        with att:
            QE = [alloc(att, f"QE{i}", [P, H, T]) for i in range(2)]
            Wq5 = alloc(att, "Wq5", [P, 5, C])
            Wv = alloc(att, "Wv", [P, C])
            Wp = alloc(att, "Wp", [P, C])
            RP = alloc(att, "RP", [P, 4, T])
            CAUS = alloc(att, "CAUS", [P, HG, P])
            SAME = alloc(att, "SAME", [P, P])
            HMEAN = alloc(att, "HMEAN", [P, P])
            ONEHOT = alloc(att, "ONEHOT", [P, H])
            GN = alloc(att, "GN", [P, 2])
            qT = [alloc(att, f"qT{i}", [P, T]) for i in range(2)]
            kT = [alloc(att, f"kT{i}", [P, T]) for i in range(2)]
            ktok = [alloc(att, f"ktok{i}", [P, NC, C]) for i in range(2)]
            V = [alloc(att, f"V{i}", [P, NC, C]) for i in range(2)]
            VE = [alloc(att, f"VE{i}", [P, NC, HG, C]) for i in range(2)]
            PR = alloc(att, "PR", [P, 8, HG, P])
            t1 = alloc(att, "t1", [P, T])
            t2 = alloc(att, "t2", [P, T])
            SG = [alloc(att, f"SG{i}", [P, T]) for i in range(2)]
            Ysb = alloc(att, "Ysb", [P, T])
            og = alloc(att, "og", [P, T])
            STsb = alloc(att, "STsb", [P, NC, C])
            gs6 = alloc(att, "gs6", [P, 6])
            gmv = alloc(att, "gmv", [P, 2])
            gst = alloc(att, "gst", [P, 2])
            gsm = alloc(att, "gsm", [P, 8])
        W1raw, W3raw = QE[0][:, 8:12, :], QE[0][:, 12:16, :]
        W2raw = VE[0][:].rearrange("p c i h -> p (c i) h")

        W2 = [alloc(ctx, f"W2{s}", [P, NCH, C], F32R) for s in ("hi", "lo")]
        hs = [[alloc(ctx, f"h{s}{i}", [P, F], F32R) for s in ("hi", "lo")] for i in range(4)]
        rows = alloc(ctx, "rows", [P, 56, NS])
        BC4 = alloc(ctx, "BC4", [P, 4, NS])
        DD = alloc(ctx, "DD", [P, 1])
        DT = alloc(ctx, "DT", [P, 1])
        L2 = alloc(ctx, "L2", [P, B, 2, NS])
        tmp = alloc(ctx, "tmp", [P, B, 2, NS])
        K = alloc(ctx, "K", [P, B])
        xs.append([alloc(ctx, f"x{s}1", [P, T], F32R) for s in ("hi", "lo")])
        hf = [alloc(ctx, f"hf{i}", [P, T]) for i in range(2)]
        sa = [alloc(ctx, f"sa{i}", [P, T]) for i in range(2)]
        oacc = alloc(ctx, "oacc", [P, T])
        otmp = alloc(ctx, "otmp", [P, T])
        GB.append(alloc(ctx, "GB1", [P, T, E]))
        xns = [alloc(ctx, f"xns{i}", [P, NC, C]) for i in range(2)]
        XT = alloc(ctx, "XT", [P, B, T])
        DK = alloc(ctx, "DK", [P, B, P])
        sst = alloc(ctx, "sst", [P, 2, NC, 6])
        smv = alloc(ctx, "smv", [P, 2, NC, 2])
        sve = alloc(ctx, "sve", [P, 2, NC])
        srs = alloc(ctx, "srs", [P, 2, NC])

        x_first, x_second, x_rest = sem("x_first"), sem("x_second"), sem("x_rest")
        att_in, rope_in, late_in, w_in, ffn_in, par_in = (
            sem("att_in"), sem("rope_in"), sem("late_in"), [sem(f"w_in{i}") for i in range(3)], sem("ffn_in"), sem("par_in"))
        half_set, zero_set, ve_zero, euler_set = (
            sem("half_set"), sem("zero_set"), sem("ve_zero"), sem("euler_set"))
        w_hi, w_lo = sem("w_hi"), sem("w_lo")
        dve_own, pool_own = sem("dve_own"), sem("pool_own")
        a_ve, a_rs, a_xn = sem("a_variance"), sem("a_rstd"), sem("a_normed")
        KINDS = {"T": 1, "q": 1, "k": 1, "v": 1, "kt": 1, "gn": 0, "proj": 0, "qs": 0, "ks": 0, "g": 0}
        made = {kind: sem(f"made_{kind}") for kind in KINDS}
        rope_done, gn_read = sem("rope_done"), sem("gn_read")
        xnT_ready, qk_ready, v_ready, ktok_ready, sg_ready = (
            sem("xnT_ready"), sem("qk_ready"), sem("v_ready"), sem("ktok_ready"), sem("sg_ready"))
        qe_act, qe_pool = sem("qe_act"), sem("qe_pool")
        sc_ready, sc_copied, p_dve, p_pool, pv_done = (
            sem("sc_ready"), sem("sc_copied"), sem("p_dve"), sem("p_pool"), sem("pv_done"))
        st_ready, st_sb, y_sb = sem("st_ready"), sem("st_sb"), sem("y_sb")
        gm_ready, gv_ready, gr_ready, og_ready, x1_done = (
            sem("gm_ready"), sem("gv_ready"), sem("gr_ready"), sem("og_ready"), sem("x1_done"))
        k_ready, dk_ready = sem("k_ready"), sem("dk_ready")
        s_ve, s_rs, s_xn, s_T, s_xT = (
            sem("s_variance"), sem("s_rstd"), sem("s_normed"), sem("s_T"), sem("s_xT"))
        s_y, x3_done = sem("s_y"), sem("x3_done")
        stored = sem("stored")

        def mixture_sems(tag):
            names = "ve rs xn T xT xs lg lr ld le gates gst gld a b sa h hi lo o og os ob xd".split()
            return {n: sem(f"m{tag}_{n}") for n in names}

        mix = [mixture_sems(1), mixture_sems(2)]

        def read_of(kind, m):
            return {"T": (xnT_ready, m + 1), "v": (v_ready, 5 * m + 5), "kt": (ktok_ready, m + 1),
                    "q": (rope_done, 4 * m + 1), "qs": (rope_done, 4 * m + 2),
                    "k": (rope_done, 4 * m + 3), "ks": (rope_done, 4 * m + 4),
                    "g": (sg_ready, m + 1), "gn": (gn_read, m + 1), "proj": (x1_done, m + 1)}[kind]

        def free_for(eng, kind, m):
            known = isinstance(m, int)
            before = {"q": "T", "k": "q", "v": "k", "kt": "v", "proj": "gn", "ks": "qs", "g": "ks"}
            if kind in before:
                eng.wait_ge(*read_of(before[kind], m))
            elif kind == "T" and not (known and m == 0):
                eng.wait_ge(*read_of("kt", m - 1))
            elif kind == "qs" and not (known and m < 2):
                eng.wait_ge(*read_of("proj", m - 2))
            elif kind == "qs" and m == 1:
                eng.wait_ge(*read_of("g", 0))
            elif kind == "gn":
                last = known and m == B - 1
                eng.wait_ge(*(read_of("proj", m - 1) if last else read_of("g", m + 1)))
            return bank[6 + KINDS[kind]]

        def ready_for(eng, kind, m):
            eng.wait_ge(made[kind], m + 1)
            return bank[6 + KINDS[kind]]

        def wait_apart(eng, semaphore, value):
            if not isinstance(value, int):
                value = eng.to_reg(value)
                eng.wait_ge(x_first, 16)
            eng.wait_ge(semaphore, value)

        def batch(m):
            return X[:, m:m + 1] if isinstance(m, int) else X[:, bass.ds(m, 1)]

        def tiles(m):
            return [batch(m)[:, 0, c, :] for c in range(NC)]

        def begun(i, n):
            return not (isinstance(i, int) and i < n)

        block = ctx.enter_context(nc.Block())

        @block.sync
        def _(sp):
            xv = x.rearrange("b (c p) h -> p b c h", p=P)
            sp.dma_start(X[:, 0], xv[:, 0]).then_inc(x_first, 16)
            for dst, src in ((ID[:], ident), (Wq5[:], w5)):
                sp.dma_start(dst, src).then_inc(att_in, 16)
            for dst, src in ((RP[:], rope), (ONEHOT[:], onehot), (Wv[:], wv)):
                sp.dma_start(dst, src).then_inc(rope_in, 16)
            late = ((CAUS[:], causal), (SAME[:], same_head), (HMEAN[:], head_mean), (Wp[:], wp),
                    (GN[:], gn))
            for dst, src in late:
                sp.dma_start(dst, src).then_inc(late_in, 16)
            assert 16 * len(late) == LATE
            sp.dma_start(X[:, 1], xv[:, 1]).then_inc(x_second, 16)
            for b in range(2, B):
                sp.dma_start(X[:, b], xv[:, b]).then_inc(x_rest, 16)
            sp.wait_ge(zero_set, 1)
            sp.dma_start(RW[:, 0:E], rw).then_inc(ffn_in, 16)
            sp.dma_start(RB[:, 0, :], rb.partition_broadcast(P)).then_inc(ffn_in, 16)
            sp.dma_start(LOWER[:], lower).then_inc(ffn_in, 16)
            sp.wait_ge(sc_ready, 16 * (B - 1))
            sp.dma_start(W1raw, w1.rearrange("e d f -> d e f")).then_inc(w_in[0], 16)
            sp.dma_start(W3raw, w3.rearrange("e d f -> d e f")).then_inc(w_in[1], 16)
            sp.wait_ge(pv_done, NC * (B - 1))
            sp.dma_start(W2raw, w2.rearrange("e (m f) d -> f (e m) d", f=P)).then_inc(w_in[2], 16)

            def gates_out(s, m, p):
                sp.wait_ge(s["gates"], m + 1)
                row = gate_rows[0, p]
                sp.dma_start(row.rearrange("(c q e) -> q c e", c=NC, e=E), G[:]).then_inc(s["gst"], 16)
                sp.wait_ge(s["gst"], 16 * (m + 1))
                sp.dma_start(GB[p][:].rearrange("q t e -> q (t e)"),
                             row.partition_broadcast(P)).then_inc(s["gld"], 16)

            def gates(s, between):
                gates_out(s, 0, 0)
                between()
                gates_out(s, 1, 1)
                with sp.Fori(0, (B - 2) // 2) as j:
                    gates_out(s, 2 * j + 2, 0)
                    gates_out(s, 2 * j + 3, 1)

            def s4d_parts():
                sp.wait_ge(sc_ready, 16 * B)
                parts = ((DT[:], log_dt), (rows[:, 0], log_a), (rows[:, 1], a_im),
                         (BC4[:, 0:2], bc), (BC4[:, 2:4], cc),
                         (DD[:], dd.rearrange("(h o) -> h o", o=1)))
                for dst, src in parts:
                    sp.dma_start(dst, src).then_inc(par_in, 16)
                assert 16 * len(parts) == PARTS

            gates(mix[0], s4d_parts)
            gates(mix[1], lambda: None)
            ov = out.rearrange("b (c p) h -> p b c h", p=P)
            for b in range(B):
                sp.wait_ge(mix[1]["xd"], b + 1)
                sp.dma_start(ov[:, b], X[:, b]).then_inc(stored, 16)
            sp.wait_ge(stored, 16 * B)

        @block.tensor
        def _(pe):
            def front_T(m, p):
                pe.wait_ge(a_xn, m + 1)
                ps = free_for(pe, "T", m)
                for c in range(NC):
                    mm = pe.transpose(ps[:, c * P:(c + 1) * P], xn[:, c, :], ID[:])
                mm.then_inc(made["T"], 1)

            def project(kind, i, m, p):
                ps = free_for(pe, kind, m)
                pe.wait_ge(xnT_ready, m + 1)
                pe.matmul(ps[:], Wq5[:, i, :], xnT[:], start=True, stop=True).then_inc(made[kind], 1)

            def project_v(m, p):
                ps = free_for(pe, "v", m)
                for c in range(NC):
                    mm = pe.matmul(ps[:, c * P:(c + 1) * P], xnT[:, c * P:(c + 1) * P], Wv[:],
                                   start=True, stop=True)
                mm.then_inc(made["v"], 1)

            def front_kt(m, p):
                ps = free_for(pe, "kt", m)
                pe.wait_ge(qk_ready, 2 * m + 2)
                for c in range(NC):
                    mm = pe.transpose(ps[:, c * P:(c + 1) * P], kT[p][:, c * P:(c + 1) * P], ID[:])
                mm.then_inc(made["kt"], 1)

            def scores(n, p, s):
                c, hg = divmod(s, HG)
                if c == 0:
                    pe.wait_ge(qe_act, 12 * n + 3 * hg + 3)
                    pe.wait_ge(qe_pool, 4 * n + hg + 1)
                k = 4 * n + c
                if begun(k, 1):
                    if hg < 3:
                        pe.wait_ge(p_dve, 3 * (k - 1) + hg + 1)
                    else:
                        pe.wait_ge(sc_copied, k)
                for j in range(P // 32):
                    cols = slice(c * P + 32 * j, (c + 1) * P)
                    dst = bank[hg][32 * j:32 * j + 32, :].rearrange("s (i t) -> s i t", i=HG)
                    mm = pe.matmul(dst[:, :, 32 * j:], kT[p][:, c * P + 32 * j:c * P + 32 * j + 32],
                                   QE[p][:, 4 * hg:4 * hg + 4, cols], start=True, stop=True)
                mm.then_inc(sc_ready, 1)

            def state(n, p, c):
                pe.wait_ge(ktok_ready, n + 1)
                if begun(3 * n + c, 1):
                    pe.wait_ge(st_sb, 3 * n + c)
                pe.matmul(bank[5][:, 0:C], ktok[p][:, c, :], V[p][:, c, :], start=(c == 0),
                          stop=(c == 2), skip_group_check=True).then_inc(st_ready, 1)

            def mix_v(n, p, c):
                cs = slice(c * P, (c + 1) * P)
                if c == 0 and begun(n, 1):
                    pe.wait_ge(y_sb, n)
                if c:
                    pe.wait_ge(st_sb, 3 * n + c)
                    pe.matmul(bank[4][:, cs], STsb[:, c, :], qT[p][:, cs], start=True, stop=False,
                              skip_group_check=True)
                pe.wait_ge(p_dve, 12 * n + 3 * c + 3)
                pe.wait_ge(p_pool, 4 * n + c + 1)
                for i in range(HG):
                    for hg in range(HG):
                        mm = pe.matmul(bank[4][32 * hg:32 * hg + 32, cs],
                                       VE[p][:, c, i, 32 * hg:32 * hg + 32],
                                       PR[:, (4 * c + hg) % 8, i, :],
                                       start=(c == 0 and i == 0), stop=(i == HG - 1),
                                       skip_group_check=True)
                mm.then_inc(pv_done, 1)

            def group_mean(m):
                pe.wait_ge(gm_ready, m + 1)
                ps = free_for(pe, "gn", m)
                pe.matmul(ps[:, 0:2], HMEAN[:], gmv[:], start=True, stop=True).then_inc(made["gn"], 1)

            def project_out(m):
                pe.wait_ge(og_ready, m + 1)
                ps = free_for(pe, "proj", m)
                for c in range(NC):
                    mm = pe.matmul(ps[:, c * P:(c + 1) * P], og[:, c * P:(c + 1) * P], Wp[:],
                                   start=True, stop=True)
                mm.then_inc(made["proj"], 1)

            def step(n, p, front=True, tail=True, beside={}):
                q = 1 - p
                for s in range(16):
                    scores(n, p, s)
                    if s in (4, 7, 10):
                        state(n, p, s // 3 - 1)
                    if s == 1 and tail:
                        mix_v(n - 1, q, 3)
                    if s == 4 and tail:
                        group_mean(n - 1)
                    if s == 5:
                        if front:
                            front_T(n + 1, q)
                        mix_v(n, p, 0)
                    if s == 8 and tail:
                        project_out(n - 1)
                    if s == 9:
                        mix_v(n, p, 1)
                    if s == 13:
                        mix_v(n, p, 2)
                    if front:
                        for at, kind, i in ((7, "q", 0), (9, "qs", 1), (10, "k", 2), (11, "ks", 3),
                                            (13, "g", 4)):
                            if s == at:
                                project(kind, i, n + 1, q)
                        if s == 12:
                            project_v(n + 1, q)
                        if s == 14:
                            front_kt(n + 1, q)
                    if s in beside:
                        beside[s]()

            def mixture(s):
                def tile_T(m):
                    pe.wait_ge(s["xn"], m + 1)
                    if begun(m, 1):
                        pe.wait_ge(s["lr"], m)
                    for c in range(NC):
                        mm = pe.transpose(bank[7][:, c * P:(c + 1) * P], xn[:, c, :], ID[:])
                    mm.then_inc(s["T"], 1)

                def logits(m):
                    pe.wait_ge(s["xT"], m + 1)
                    for c in range(NC):
                        mm = pe.matmul(bank[7][:, c * P:(c + 1) * P], xnT[:, c * P:(c + 1) * P],
                                       RW[:], start=True, stop=True)
                    mm.then_inc(s["lg"], 1)

                def split_product(ps, w, cols, v, start, stop):
                    for a, (i, j) in enumerate(((0, 0), (0, 1), (1, 0))):
                        mm = pe.matmul(ps[:], w[i][cols], v[j][:], start=(start and a == 0),
                                       stop=(stop and a == 2))
                    return mm

                def up(n, p, k):
                    e, m = divmod(k, FC)
                    cols = (slice(None), e, slice(m * P, (m + 1) * P))
                    i = NCH * n + k
                    if begun(i, 2):
                        pe.wait_ge(s["sa"], i - 1)
                    split_product(bank[k % 2], W1, cols, xs[p], True, True).then_inc(s["a"], 1)
                    if begun(i, 2):
                        pe.wait_ge(s["h"], i - 1)
                    split_product(bank[2 + k % 2], W3, cols, xs[p], True, True).then_inc(s["b"], 1)

                def down(n, k):
                    e, m = divmod(k, FC)
                    if m == 0 and begun(4 * n + e, 2):
                        pe.wait_ge(s["og"], 4 * n + e - 1)
                    pe.wait_ge(s["lo"], NCH * n + k + 1)
                    mm = split_product(bank[4 + e % 2], W2, (slice(None), k, slice(None)), hs[k % 4],
                                       m == 0, m == FC - 1)
                    if m == FC - 1:
                        mm.then_inc(s["o"], 1)

                def tile_back(m):
                    pe.wait_ge(s["os"], m + 1)
                    for c in range(NC):
                        mm = pe.transpose(bank[6][:, c * P:(c + 1) * P],
                                          oacc[:, c * P:(c + 1) * P], ID[:])
                    mm.then_inc(s["ob"], 1)

                def step(n, p, front=True, tail=True, beside={}):
                    pe.wait_ge(s["xs"], 2 * n + 2)
                    for k in range(NCH):
                        up(n, p, k)
                        if k >= BEHIND:
                            down(n, k - BEHIND)
                        elif tail:
                            down(n - 1, NCH - BEHIND + k)
                        if k == 5 and tail:
                            tile_back(n - 1)
                        if k == 6 and front:
                            tile_T(n + 1)
                        if k == 10 and front:
                            logits(n + 1)
                        if k in beside:
                            beside[k]()

                return tile_T, logits, down, tile_back, step

            def turn(b):
                pe.wait_ge(s_xn, b + 1)
                if b:
                    pe.wait_ge(s_xT, b)
                for c in range(NC):
                    mm = pe.transpose(bank[7][:, c * P:(c + 1) * P], xns[b % 2][:, c, :], ID[:])
                mm.then_inc(s_T, 1)

            def convolve(b):
                pe.wait_ge(s_xT, b + 1)
                if b == 0:
                    pe.wait_ge(dk_ready, 1)
                    pe.wait_ge(mix[0]["sa"], NCH * B)
                if b >= 2:
                    pe.wait_ge(x3_done, b - 1)
                for c in range(NC):
                    cs = slice(c * P, (c + 1) * P)
                    for l in range(b + 1):
                        mm = pe.matmul(bank[b % 2][:, cs], XT[:, b - l, cs], DK[:, l, :],
                                       start=(l == 0), stop=(l == b))
                mm.then_inc(s_y, 1)

            T1, logits1, down1, back1, step1 = mixture(mix[0])
            T2, logits2, down2, back2, step2 = mixture(mix[1])

            pe.wait_ge(att_in, 32)
            front_T(0, 0)
            for kind, i in (("q", 0), ("qs", 1), ("k", 2), ("ks", 3)):
                project(kind, i, 0, 0)
            pe.wait_ge(rope_in, 48)
            project_v(0, 0)
            project("g", 4, 0, 0)
            front_kt(0, 0)
            pe.wait_ge(ve_zero, 2)
            pe.wait_ge(v_ready, 5)
            pe.wait_ge(late_in, LATE)
            pe.wait_ge(zero_set, 5)
            steps(pe, None, lambda: step(0, 0, tail=False), step,
                  lambda: step(B - 1, 1, front=False, beside={6: lambda: T1(0), 10: lambda: logits1(0)}))
            mix_v(B - 1, 1, 3)

            pe.wait_ge(w_lo, 3)
            steps(pe, None, lambda: step1(0, 0, tail=False, beside={
                1: lambda: group_mean(B - 1), 4: lambda: project_out(B - 1)}), step1,
                lambda: step1(B - 1, 1, front=False, beside={
                    6: lambda: turn(0), 10: lambda: turn(1), 13: lambda: turn(2)}))

            down1(B - 1, NCH - 3)
            down1(B - 1, NCH - 2)
            convolve(0)
            down1(B - 1, NCH - 1)
            turn(3)
            convolve(1)
            turn(4)
            convolve(2)
            back1(B - 1)
            turn(5)
            convolve(3)
            turn(6)
            convolve(4)
            turn(7)
            convolve(5)
            pe.wait_ge(s_xT, B)
            T2(0)
            convolve(6)
            logits2(0)
            convolve(7)

            pe.wait_ge(x3_done, B)
            steps(pe, None, lambda: step2(0, 0, tail=False), step2,
                  lambda: step2(B - 1, 1, front=False))
            down2(B - 1, NCH - 3)
            down2(B - 1, NCH - 2)
            down2(B - 1, NCH - 1)
            back2(B - 1)

        @block.scalar
        def _(act):
            def spread(m, p, k):
                hg, i = divmod(k, 3)
                h = 4 * hg + (0, 2, 3)[i]
                if k == 0:
                    act.wait_ge(qk_ready, 2 * m + 1)
                nc.scalar.activation(QE[p][:, h, :], qT[p][:], ACT.Copy,
                                     scale=ONEHOT[:, h:h + 1]).then_inc(qe_act, 1)

            def copy_T(m):
                ps = ready_for(act, "T", m)
                nc.scalar.activation(xnT[:], ps[:], ACT.Copy).then_inc(xnT_ready, 1)

            def copy_v(m, p):
                ps = ready_for(act, "v", m)
                nc.scalar.activation(V[p][:].rearrange("p c h -> p (c h)"), ps[:], ACT.Copy)\
                    .then_inc(v_ready, 1)
                pv = ps[:].rearrange("p (c g i d) -> p c g i d", c=NC, g=HG, i=HG)
                vv = VE[p][:].rearrange("p c i (g j d) -> p c i g j d", g=HG, j=HG)
                for i in range(HG):
                    nc.scalar.activation(vv[:, :, i, :, i, :], pv[:, :, :, i, :], ACT.Copy)\
                        .then_inc(v_ready, 1)

            def gate(m, p):
                ps = ready_for(act, "g", m)
                nc.scalar.activation(SG[p][:], ps[:], ACT.Silu).then_inc(sg_ready, 1)

            def copy_kt(m, p):
                ps = ready_for(act, "kt", m)
                nc.scalar.activation(ktok[p][:].rearrange("p c h -> p (c h)"), ps[:], ACT.Copy)\
                    .then_inc(ktok_ready, 1)

            def copy_scores(n, c):
                k = 4 * n + c
                if begun(k, 2):
                    act.wait_ge(pv_done, k - 1)
                act.wait_ge(sc_ready, 16 * n + 4 * c + 4)
                nc.scalar.activation(PR[:, (4 * c + 3) % 8].rearrange("p i t -> p (i t)"), bank[3][:],
                                     ACT.Copy).then_inc(sc_copied, 1)

            def read_y(m):
                act.wait_ge(pv_done, 4 * m + 4)
                nc.scalar.activation(Ysb[:], bank[4][:], ACT.Copy).then_inc(y_sb, 1)

            def step(n, p, front=True, tail=True, beside={}):
                q = 1 - p
                if tail:
                    read_y(n - 1)
                copy_scores(n, 0)
                if front:
                    copy_T(n + 1)
                if 0 in beside:
                    beside[0]()
                copy_scores(n, 1)
                if 1 in beside:
                    beside[1]()
                if front:
                    for k in range(3):
                        spread(n + 1, q, k)
                copy_scores(n, 2)
                if 2 in beside:
                    beside[2]()
                if front:
                    for k in range(3, 6):
                        spread(n + 1, q, k)
                    copy_v(n + 1, q)
                    gate(n + 1, q)
                copy_scores(n, 3)
                if front:
                    for k in range(6, 12):
                        spread(n + 1, q, k)
                    copy_kt(n + 1, q)

            def first():
                copy_T(0)
                for k in range(12):
                    spread(0, 0, k)
                    if k == 2:
                        copy_v(0, 0)
                        gate(0, 0)
                        copy_kt(0, 0)
                step(0, 0, tail=False)

            def high(i, dst, raw):
                act.wait_ge(w_in[i], 16)
                nc.scalar.activation(dst[0][:], raw, ACT.Copy).then_inc(w_hi, 1)

            def mixture(s):
                def front(m):
                    act.wait_ge(s["T"], m + 1)
                    if begun(m, 1):
                        act.wait_ge(s["xs"], 2 * m)
                        act.wait_ge(s["lg"], m)
                    nc.scalar.activation(xnT[:], bank[7][:], ACT.Copy).then_inc(s["xT"], 1)

                def hidden_high(i, k):
                    act.wait_ge(s["h"], i + 1)
                    nc.scalar.activation(hs[k % 4][0][:], hf[k % 2][:], ACT.Copy).then_inc(s["hi"], 1)

                def step(n, p, front_=True, beside={}):
                    for k in range(NCH):
                        i = NCH * n + k
                        act.wait_ge(s["a"], i + 1)
                        if begun(i, 2):
                            act.wait_ge(s["h"], i - 1)
                        nc.scalar.activation(sa[k % 2][:], bank[k % 2][:], ACT.Silu)\
                            .then_inc(s["sa"], 1)
                        if begun(i, 1):
                            hidden_high(i - 1, (k - 1) % NCH)
                        if k == 7 and front_:
                            front(n + 1)
                        if k in beside:
                            beside[k]()

                return front, hidden_high, step

            def turned(b):
                act.wait_ge(s_T, b + 1)
                nc.scalar.activation(XT[:, b, :], bank[7][:], ACT.Copy).then_inc(s_xT, 1)

            front1, high1, step1 = mixture(mix[0])
            front2, high2, step2 = mixture(mix[1])
            act.wait_ge(rope_in, 48)
            act.wait_ge(ve_zero, 2)
            steps(act, None, first, step, lambda: step(B - 1, 1, front=False, beside={
                0: lambda: high(0, W1, W1raw), 1: lambda: (front1(0), high(1, W3, W3raw)),
                2: lambda: high(2, W2, W2raw)}))
            read_y(B - 1)
            steps(act, None, lambda: step1(0, 0), step1, lambda: step1(B - 1, 1, False, beside={
                7: lambda: turned(0), 11: lambda: turned(1), 14: lambda: turned(2)}))
            high1(NCH * B - 1, NCH - 1)
            for b in range(3, B):
                turned(b)
            front2(0)
            steps(act, None, lambda: step2(0, 0), step2, lambda: step2(B - 1, 1, False))
            high2(NCH * B - 1, NCH - 1)

        @block.vector
        def _(dve):
            own = Own(dve, dve_own)
            tt, ts, stt = nc.vector.tensor_tensor, nc.vector.tensor_scalar, nc.vector.scalar_tensor_tensor

            def norm_stats(src, st, mv_, ve, ready):
                for c in range(NC):
                    own.did(nc.vector.bn_stats(st[:, c, :], src[c]))
                wait_apart(dve, dve_own, own.base + own.k)
                for c in range(NC):
                    own.did(nc.vector.bn_aggr(mv_[:, c, :], st[:, c, :]))
                own.wait()
                ts(ve, mv_[:, :, 1], EPS, None, ALU.add).then_inc(ready, 1)

            def norm_apply(dst, src, mv_, rs, done):
                for c in range(NC):
                    a = ts(dst[:, c, :], src[c], mv_[:, c, 0:1], rs[:, c:c + 1],
                           ALU.subtract, ALU.mult)
                a.then_inc(done, 1)

            def a_stats(m):
                if isinstance(m, int):
                    dve.wait_ge(*[(x_first, 16), (x_second, 16)][m])
                norm_stats(tiles(m), stats, mv, veps[:], a_ve)

            def a_apply(m):
                dve.wait_ge(a_rs, m + 1)
                if begun(m, 1):
                    dve.wait_ge(made["T"], m)
                norm_apply(xn, tiles(m), mv, rstd, a_xn)

            def rope_half(m, p, kind, i, dst):
                ps = ready_for(dve, kind, m)
                if kind == "q" and begun(m, 2):
                    dve.wait_ge(og_ready, m - 1)
                if kind == "k":
                    dve.wait_ge(qk_ready, 2 * m + 1)
                tt(dst[:], ps[:], RP[:, i, :], ALU.mult).then_inc(rope_done, 1)

            def rope_add(m, dst, i):
                dve.wait_ge(rope_done, 4 * m + 2 * i + 2)
                tt(dst[:], t1[:], t2[:], ALU.add).then_inc(qk_ready, 1)

            def mask(n, p, s):
                c, hg = divmod(s, HG)
                if hg == 3:
                    return
                if hg == 0 and begun(4 * n + c, 2):
                    dve.wait_ge(pv_done, 4 * n + c - 1)
                dve.wait_ge(sc_ready, 16 * n + s + 1)
                tt(PR[:, s % 8], bank[hg][:].rearrange("p (i t) -> p i t", i=HG), CAUS[:],
                   ALU.mult).then_inc(p_dve, 1)

            def state(n, p, c):
                dve.wait_ge(st_ready, 3 * n + c)
                if begun(n, 1):
                    dve.wait_ge(pv_done, 4 * (n - 1) + c + 1)
                tt(STsb[:, c, :], bank[5][:, 0:C], SAME[:], ALU.mult).then_inc(st_sb, 1)

            def group_a(m):
                dve.wait_ge(y_sb, m + 1)
                own.did(nc.vector.bn_stats(gs6[:], Ysb[:]))
                wait_apart(dve, dve_own, own.base + own.k)
                own.link(nc.vector.bn_aggr(gmv[:], gs6[:]))
                stt(out=gmv[:, 1:2], in0=gmv[:, 0:1], scalar=gmv[:, 0:1], in1=gmv[:, 1:2],
                    op0=ALU.mult, op1=ALU.add).then_inc(gm_ready, 1)

            def group_b(m):
                ps = ready_for(dve, "gn", m)
                nc.vector.tensor_copy(gst[:], ps[:, 0:2]).then_inc(gn_read, 1)
                dve.wait_ge(gn_read, m + 1)
                own.link(stt(out=gsm[:, 0:1], in0=gst[:, 0:1], scalar=gst[:, 0:1], in1=gst[:, 1:2],
                             op0=ALU.mult, op1=ALU.subtract))
                ts(gsm[:, 1:2], gsm[:, 0:1], -1.0, EPS, ALU.mult, ALU.add).then_inc(gv_ready, 1)

            def group_c(m, p):
                dve.wait_ge(gr_ready, m + 1)
                own.link(tt(gsm[:, 3:4], gsm[:, 2:3], GN[:, 0:1], ALU.mult))
                own.link(stt(out=gsm[:, 4:5], in0=gst[:, 0:1], scalar=gsm[:, 3:4], in1=GN[:, 1:2],
                             op0=ALU.mult, op1=ALU.subtract))
                dve.wait_ge(sg_ready, m + 1)
                own.link(ts(t1[:], Ysb[:], gsm[:, 3:4], gsm[:, 4:5], ALU.mult, ALU.subtract))
                tt(og[:], t1[:], SG[p][:], ALU.mult).then_inc(og_ready, 1)

            def add_to_x(m, ps, done):
                xb = batch(m).rearrange("p o c h -> p (o c h)")
                tt(xb, ps[:], xb, ALU.add).then_inc(done, 1)

            def residual(m):
                add_to_x(m, ready_for(dve, "proj", m), x1_done)

            def step(n, p, front=True, tail=True, beside={}):
                q = 1 - p
                for s in range(16):
                    mask(n, p, s)
                    if s == 0 and front:
                        a_stats(n + 1)
                    if s in (5, 8, 11):
                        state(n, p, s // 3)
                    if s == 2 and tail:
                        group_a(n - 1)
                    if s == 3 and front:
                        a_apply(n + 1)
                    if s == 5 and tail:
                        group_b(n - 1)
                    if s == 6 and tail:
                        group_c(n - 1, q)
                    if s == 8 and tail:
                        residual(n - 1)
                    if front:
                        if s == 7:
                            rope_half(n + 1, q, "q", 0, t1)
                        if s == 9:
                            rope_half(n + 1, q, "qs", 1, t2)
                            rope_add(n + 1, qT[q], 0)
                        if s == 10:
                            rope_half(n + 1, q, "k", 2, t1)
                        if s == 11:
                            rope_half(n + 1, q, "ks", 3, t2)
                            rope_add(n + 1, kT[q], 1)
                    if s in beside:
                        beside[s]()

            def first():
                a_stats(0)
                a_apply(0)
                dve.wait_ge(rope_in, 48)
                rope_half(0, 0, "q", 0, t1)
                rope_half(0, 0, "qs", 1, t2)
                rope_add(0, qT[0], 0)
                rope_half(0, 0, "k", 2, t1)
                rope_half(0, 0, "ks", 3, t2)
                rope_add(0, kT[0], 1)
                dve.wait_ge(late_in, LATE)
                step(0, 0, tail=False)
                dve.wait_ge(x_rest, 16 * (B - 2))

            def low_part(i, dst, raw):
                dve.wait_ge(w_hi, i + 1)
                tt(dst[1][:], raw, dst[0][:].bitcast(F32), ALU.subtract).then_inc(w_lo, 1)

            def mixture(s):
                def m_stats(m):
                    norm_stats(tiles(m), stats, mv, veps[:], s["ve"])

                def m_apply(m):
                    dve.wait_ge(s["rs"], m + 1)
                    if begun(m, 1):
                        dve.wait_ge(s["T"], m)
                    norm_apply(xn, tiles(m), mv, rstd, s["xn"])

                def split_x(m, p):
                    dve.wait_ge(s["xT"], m + 1)
                    if begun(m, 2):
                        dve.wait_ge(s["b"], NCH * (m - 1))
                    nc.vector.tensor_copy(xs[p][0][:], xnT[:]).then_inc(s["xs"], 1)
                    dve.wait_ge(s["xs"], 2 * m + 1)
                    tt(xs[p][1][:], xnT[:], xs[p][0][:].bitcast(F32), ALU.subtract)\
                        .then_inc(s["xs"], 1)

                def route_a(m):
                    dve.wait_ge(s["lg"], m + 1)
                    tt(LG[:], bank[7][:].rearrange("p (c e) -> p c e", c=NC)[:, :, 0:E],
                       RB[:].to_broadcast([P, NC, E]), ALU.add).then_inc(s["lr"], 1)
                    dve.wait_ge(s["lr"], m + 1)
                    own.link(nc.vector.tensor_reduce(mx[:], LG[:], AX_X, ALU.max))
                    tt(LD[:], LG[:], mx[:].unsqueeze(2).to_broadcast([P, NC, E]), ALU.subtract)\
                        .then_inc(s["ld"], 1)

                def route_b(m, part):
                    if part == 0:
                        lj = LG[:].unsqueeze(2).to_broadcast([P, NC, E, E])
                        li = LG[:].unsqueeze(3).to_broadcast([P, NC, E, E])
                        own.did(tt(GT[:], lj, li, ALU.is_gt))
                        own.link(tt(EQ[:], lj, li, ALU.is_equal))
                        own.link(tt(EQ[:], EQ[:], LOWER[:], ALU.mult))
                        own.link(tt(GT[:], GT[:], EQ[:], ALU.add))
                        own.did(nc.vector.tensor_reduce(rank[:], GT[:], AX_X, ALU.add))
                        return
                    own.wait()
                    own.link(ts(rank[:], rank[:], 1.5, None, ALU.is_lt))
                    dve.wait_ge(s["le"], m + 1)
                    own.link(tt(pm[:], LE[:], rank[:], ALU.mult))
                    own.link(nc.vector.tensor_reduce(smr[:], pm[:], AX_X, ALU.add))
                    own.link(nc.vector.reciprocal(smr[:], smr[:]))
                    if begun(m, 1):
                        dve.wait_ge(s["gst"], 16 * m)
                    tt(G[:], pm[:], smr[:].unsqueeze(2).to_broadcast([P, NC, E]), ALU.mult)\
                        .then_inc(s["gates"], 1)

                def hidden(i, k):
                    dve.wait_ge(s["sa"], i + 1)
                    dve.wait_ge(s["b"], i + 1)
                    if begun(i, 2):
                        dve.wait_ge(s["lo"], i - 1)
                    tt(hf[k % 2][:], bank[2 + k % 2][:], sa[k % 2][:], ALU.mult).then_inc(s["h"], 1)

                def low(i, k):
                    dve.wait_ge(s["hi"], i + 1)
                    tt(hs[k % 4][1][:], hf[k % 2][:], hs[k % 4][0][:].bitcast(F32), ALU.subtract)\
                        .then_inc(s["lo"], 1)

                def gated(n, p, e):
                    if e == 0:
                        dve.wait_ge(s["gld"], 16 * (n + 1))
                        if begun(n, 1):
                            dve.wait_ge(s["ob"], n)
                    o = 4 * n + e
                    dve.wait_ge(s["o"], o + 1)
                    dst = oacc if e == 0 else otmp
                    tt(dst[:], bank[4 + e % 2][:], GB[p][:, :, e], ALU.mult).then_inc(s["og"], 1)
                    dve.wait_ge(s["og"], o + 1)
                    if e:
                        a = tt(oacc[:], oacc[:], otmp[:], ALU.add)
                        if e == E - 1:
                            a.then_inc(s["os"], 1)
                        else:
                            own.did(a)

                def residual(m):
                    dve.wait_ge(s["ob"], m + 1)
                    add_to_x(m, bank[6], s["xd"])

                def step(n, p, front=True, tail=True, beside={}):
                    q = 1 - p
                    for k in range(NCH):
                        i = NCH * n + k
                        hidden(i, k)
                        if begun(i, 1):
                            low(i - 1, (k - 1) % NCH)
                        if k in (7, 11, 15):
                            gated(n, p, k // 4 - 1)
                        if tail and k == 3:
                            gated(n - 1, q, 3)
                        if tail and k == 6:
                            residual(n - 1)
                        if front:
                            if k == 1:
                                m_stats(n + 1)
                            if k == 4:
                                m_apply(n + 1)
                            if k == 9:
                                split_x(n + 1, q)
                            if k == 12:
                                route_a(n + 1)
                            if k in (13, 14):
                                route_b(n + 1, k - 13)
                        if k in beside:
                            beside[k]()

                return m_stats, m_apply, split_x, route_a, route_b, low, gated, residual, step

            def s_stats(b):
                i = b % 2
                norm_stats(tiles(b), sst[:, i], smv[:, i], sve[:, i, :], s_ve)

            def s_apply(b):
                i = b % 2
                dve.wait_ge(s_rs, b + 1)
                if b >= 2:
                    dve.wait_ge(s_T, b - 1)
                norm_apply(xns[i], tiles(b), smv[:, i], srs[:, i], s_xn)

            def s_next(b):
                s_apply(b)
                if b + 1 < B:
                    s_stats(b + 1)

            def diagonals():
                dve.wait_ge(k_ready, 1)
                for l in range(B):
                    a = ts(DK[:, l, :], ID[:], K[:, l:l + 1], None, ALU.mult)
                a.then_inc(dk_ready, 1)

            def s_residual(b):
                dve.wait_ge(s_y, b + 1)
                add_to_x(b, bank[b % 2], x3_done)

            nc.vector.memset(half[:], -0.5).then_inc(half_set, 1)
            nc.vector.memset(RW[:], 0.0).then_inc(zero_set, 1)
            for i in range(HG):
                nc.vector.memset(bank[i][:], 0.0).then_inc(zero_set, 1)

            (m_stats1, m_apply1, split_x1, route_a1, route_b1, low1, gated1, residual1, step1) = (
                mixture(mix[0]))
            (m_stats2, m_apply2, split_x2, route_a2, route_b2, low2, gated2, residual2, step2) = (
                mixture(mix[1]))

            steps(dve, own, first, step, lambda: step(B - 1, 1, front=False, beside={
                4: lambda: m_stats1(0), 5: lambda: m_apply1(0),
                8: lambda: low_part(0, W1, W1raw), 9: lambda: split_x1(0, 0),
                10: lambda: (dve.wait_ge(ffn_in, 48), low_part(1, W3, W3raw)),
                12: lambda: route_a1(0), 13: lambda: route_b1(0, 0),
                14: lambda: route_b1(0, 1), 15: lambda: low_part(2, W2, W2raw)}))
            group_a(B - 1)
            steps(dve, own, lambda: step1(0, 0, tail=False, beside={
                2: lambda: group_b(B - 1), 3: lambda: group_c(B - 1, 1),
                5: lambda: residual(B - 1)}), step1,
                lambda: step1(B - 1, 1, front=False, beside={
                    1: lambda: s_stats(0), 4: lambda: s_next(0), 8: lambda: s_next(1),
                    9: diagonals, 12: lambda: s_next(2)}))
            low1(NCH * B - 1, NCH - 1)
            s_next(3)
            s_residual(0)
            s_next(4)
            gated1(B - 1, 1, 3)
            s_next(5)
            s_residual(1)
            residual1(B - 1)
            s_residual(2)
            s_apply(6)
            s_residual(3)
            dve.wait_ge(mix[0]["xd"], B)
            s_stats(7)
            s_apply(7)
            s_residual(4)
            dve.wait_ge(x3_done, 1)
            m_stats2(0)
            m_apply2(0)
            s_residual(5)
            split_x2(0, 0)
            s_residual(6)
            route_a2(0)
            s_residual(7)
            route_b2(0, 0)
            route_b2(0, 1)
            steps(dve, own, lambda: step2(0, 0, tail=False), step2,
                  lambda: step2(B - 1, 1, front=False))
            low2(NCH * B - 1, NCH - 1)
            gated2(B - 1, 1, 3)
            residual2(B - 1)

        @block.gpsimd
        def _(pool):
            own = Own(pool, pool_own)
            tt, ts = nc.gpsimd.tensor_tensor, nc.gpsimd.tensor_scalar

            def spread(m, p, hg):
                h = 4 * hg + 1
                if hg == 0:
                    wait_apart(pool, qk_ready, 2 * m + 1)
                ts(QE[p][:, h, :], qT[p][:], ONEHOT[:, h:h + 1], None, ALU.mult).then_inc(qe_pool, 1)

            def inverse_root(ready, k, out_, in_, n, done):
                pool.wait_ge(ready, k + 1)
                tt(out_, in_, half[:, 0:n], ALU.pow).then_inc(done, 1)

            def mask(n, c):
                pool.wait_ge(sc_copied, 4 * n + c + 1)
                pr = PR[:, (4 * c + 3) % 8]
                tt(pr, pr, CAUS[:], ALU.mult).then_inc(p_pool, 1)

            def layer_root(m):
                inverse_root(a_ve, m, rstd[:], veps[:], NC, a_rs)

            def group_root(m):
                inverse_root(gv_ready, m, gsm[:, 2:3], gsm[:, 1:2], 1, gr_ready)

            def step(n, p, front=True, tail=True, beside={}):
                if front:
                    layer_root(n + 1)
                mask(n, 0)
                if tail:
                    group_root(n - 1)
                if 0 in beside:
                    beside[0]()
                mask(n, 1)
                for c in (2, 3):
                    if front:
                        spread(n + 1, 1 - p, 2 * c - 4)
                    mask(n, c)
                    if c in beside:
                        beside[c]()
                    if front:
                        spread(n + 1, 1 - p, 2 * c - 3)

            def first():
                layer_root(0)
                for hg in range(HG):
                    spread(0, 0, hg)
                pool.wait_ge(late_in, LATE)
                step(0, 0, tail=False)

            def kernel_terms():
                pool.wait_ge(par_in, PARTS)
                free = [2]

                def new():
                    free[0] += 1
                    return rows[:, free[0] - 1, :]

                def mul(a, b):
                    o = new()
                    own.link(tt(o, a, b, ALU.mult))
                    return o

                def add(a, b, op=ALU.add, o=None):
                    o = new() if o is None else o
                    own.link(tt(o, a, b, op))
                    return o

                def lin(a, m, c):
                    o = new()
                    own.link(ts(o, a, m, c, ALU.mult, ALU.add))
                    return o

                def exp(a):
                    o = new()
                    own.link(tt(o, EULER[:], a, ALU.pow))
                    return o

                ld = new()
                own.link(nc.gpsimd.tensor_copy(ld, DT[:].to_broadcast([P, NS])))
                dt_ = exp(ld)
                zr = lin(mul(dt_, exp(rows[:, 0, :])), -0.5, 0.0)
                zi = lin(mul(dt_, rows[:, 1, :]), 0.5, 0.0)
                one = lin(zr, -1.0, 1.0)
                zi2 = mul(zi, zi)
                den = add(mul(one, one), zi2)
                minus = lin(zr, 0.0, -1.0)
                iden = new()
                own.link(tt(iden, den, minus, ALU.pow))
                ar = mul(add(lin(mul(zr, zr), -1.0, 1.0), zi2, ALU.subtract), iden)
                ai = mul(lin(zi, 2.0, 0.0), iden)
                br, bi, cr, ci = (BC4[:, i] for i in range(4))
                pr_ = add(mul(br, cr), mul(bi, ci), ALU.subtract)
                pi_ = add(mul(br, ci), mul(bi, cr))
                w = lin(mul(dt_, iden), 0.5, 0.0)
                er, ei = mul(w, one), mul(w, zi)
                add(mul(pr_, er), mul(pi_, ei), ALU.subtract, L2[:, 0, 0, :])
                add(mul(pr_, ei), mul(pi_, er), ALU.add, L2[:, 0, 1, :])
                return ar, ai, add, mul, lin

            def kernel_powers(re, im, add, mul, lin):
                for k in range(3):
                    n = 1 << k
                    low, high = L2[:, 0:n], L2[:, n:2 * n]
                    rv, iv = (v.unsqueeze(1).to_broadcast([P, n, NS]) for v in (re, im))
                    u, v = tmp[:, 0:n, 0, :], tmp[:, 0:n, 1, :]
                    own.did(tt(u, low[:, :, 1, :], iv, ALU.mult))
                    own.did(tt(v, low[:, :, 1, :], rv, ALU.mult))
                    own.did(tt(high[:, :, 0, :], low[:, :, 0, :], rv, ALU.mult))
                    own.link(tt(high[:, :, 1, :], low[:, :, 0, :], iv, ALU.mult))
                    own.did(tt(high[:, :, 0, :], high[:, :, 0, :], u, ALU.subtract))
                    own.link(tt(high[:, :, 1, :], high[:, :, 1, :], v, ALU.add))
                    if k < 2:
                        re, im = (add(mul(re, re), mul(im, im), ALU.subtract),
                                  lin(mul(re, im), 2.0, 0.0))
                w = NS // 2
                while w:
                    own.link(tt(L2[:, :, 0, 0:w], L2[:, :, 0, 0:w], L2[:, :, 0, w:2 * w], ALU.add))
                    w //= 2
                own.did(tt(K[:, 0:1], L2[:, 0, 0, 0:1], DD[:], ALU.add))
                nc.gpsimd.tensor_copy(K[:, 1:B], L2[:, 1:B, 0, 0]).then_inc(k_ready, 1)

            def mixture(s):
                def norm_root(m):
                    inverse_root(s["ve"], m, rstd[:], veps[:], NC, s["rs"])

                def exps(m):
                    pool.wait_ge(s["ld"], m + 1)
                    e16 = EULER[:, 0:NC * E].rearrange("p (c e) -> p c e", e=E)
                    tt(LE[:], e16, LD[:], ALU.pow).then_inc(s["le"], 1)

                def step(n, p):
                    norm_root(n + 1)
                    exps(n + 1)

                return norm_root, exps, step

            norm_root1, exps1, step1 = mixture(mix[0])
            norm_root2, exps2, step2 = mixture(mix[1])
            pool.wait_ge(half_set, 1)
            for v in VE:
                nc.gpsimd.memset(v[:], 0.0).then_inc(ve_zero, 1)
            nc.gpsimd.memset(EULER[:], float(np.e)).then_inc(euler_set, 1)
            pool.wait_ge(euler_set, 1)
            pool.wait_ge(rope_in, 48)
            steps(pool, None, first, step, lambda: step(B - 1, 1, front=False, beside={
                0: lambda: norm_root1(0), 3: lambda: exps1(0)}))

            def first_step():
                group_root(B - 1)
                norm_root1(1)
                terms = kernel_terms()
                exps1(1)
                kernel_powers(*terms)

            steps(pool, None, first_step, step1, lambda: None)
            for b in range(B):
                inverse_root(s_ve, b, srs[:, b % 2, :], sve[:, b % 2, :], NC, s_rs)
            norm_root2(0)
            exps2(0)
            steps(pool, None, lambda: step2(0, 0), step2, lambda: None)


def launch_arrays(inputs):
    def f(name):
        return np.ascontiguousarray(inputs[name])

    w = f("L0_attn_a_w_qkv")
    swap = np.arange(C) ^ 1
    q, k, v = w[0:C], w[C:2 * C], w[2 * C:]
    w5 = np.stack([q.T, q[swap].T, k.T, k[swap].T, f("L0_attn_a_w_gated").T], axis=1)
    arrays = {
        "x": f("L0_attn_a_x"), "w5": w5, "wv": v.T, "wp": f("L0_attn_a_w_proj").T,
        "gn": np.stack([f("L0_attn_a_gn_weight"), f("L0_attn_a_gn_bias")], axis=1),
        "log_dt": f("L0_attn_b_log_dt"), "log_a": f("L0_attn_b_log_A_real"), "a_im": f("L0_attn_b_A_imag"),
        "bc": f("L0_attn_b_B").transpose(0, 2, 1), "cc": f("L0_attn_b_C").transpose(0, 2, 1), "dd": f("L0_attn_b_D"),
        "rw": f("L0_ffn_router_w"), "rb": f("L0_ffn_router_b"),
        "w1": f("L0_ffn_w1"), "w3": f("L0_ffn_w3"), "w2": f("L0_ffn_w2"),
    }
    arrays |= constants()
    return {n: np.ascontiguousarray(a) for n, a in arrays.items()}


def kernel(**inputs):
    import concourse.bacc as bacc
    from concourse.bass_utils import run_bass_kernel_spmd

    nc = bacc.Bacc("TRN2", target_bir_lowering=False, num_devices=1)
    arrays = launch_arrays(inputs)
    args = [nc.dram_tensor(n, a.shape, mybir.dt.from_np(a.dtype), kind="ExternalInput").ap()
            for n, a in arrays.items()]
    out = nc.dram_tensor("out", (B, T, C), F32, kind="ExternalOutput").ap()
    build(nc, *args, out)
    return run_bass_kernel_spmd(nc, [arrays], core_ids=[0]).results[0]["out"]
```

```python
from contextlib import ExitStack

import numpy as np

import concourse.bass as bass
from concourse import mybir

F32 = mybir.dt.float32
F32R = mybir.dt.float32r
ALU = mybir.AluOpType
ACT = mybir.ActivationFunctionType
AX_X = mybir.AxisListType.X

P = 128
B, T, C = 8, 512, 128
NC = T // P
H, HD = 16, 8
HG = 4
E, F = 4, 512
FC = F // P
NCH = E * FC
NS = 16
EPS = 1e-5
PER_TURN = (28, 54, 38)
FIRST_HEADS = (0, 4, 5, 8, 9, 12)
BEHIND = 3
LATE, PARTS = 16 * 4, 16 * 6


def constants():
    d = np.arange(0, HD, 2, dtype=np.float64)
    inv_freq = 1.0 / 10000.0 ** (d / HD)
    t = np.arange(T, dtype=np.float64)
    scale = ((d + 0.4 * HD) / (1.4 * HD))[:, None] ** ((t - T // 2) / 512.0)[None, :]
    cos, sin = np.cos(inv_freq[:, None] * t), np.sin(inv_freq[:, None] * t)
    gamma = 1.0 - 2.0 ** (-5.0 - np.arange(H, dtype=np.float64))
    rope = np.zeros((C, 4, T))
    for c in range(C):
        h, i, odd = c // HD, c % HD // 2, c % 2
        sign = 1.0 if odd else -1.0
        up, down = gamma[h] ** t * HD ** -0.5, gamma[h] ** -t
        rope[c] = (cos[i] * scale[i] * up, sign * sin[i] * scale[i] * up,
                   cos[i] / scale[i] * down, sign * sin[i] / scale[i] * down)
    rope = rope.reshape(C, 2, 2, NC, P).transpose(4, 2, 3, 1, 0)
    i = np.arange(P)
    head = i // HD
    same = (head[:, None] == head[None, :]).astype(np.float64)
    causal = (i[:, None] <= i[None, :]).astype(np.float64)
    onehot = (head[:, None] == np.arange(H)[None, :]).astype(np.float64)
    lower = np.broadcast_to(np.tril(np.ones((E, E)), -1), (P, NC, E, E))
    tables = {
        "rope": rope, "causal": causal, "same_head": same,
        "onehot": onehot, "ident": np.eye(P), "lower": lower,
    }
    return {n: np.ascontiguousarray(a, dtype=np.float32) for n, a in tables.items()}


class Own:

    def __init__(self, eng, sem):
        self.eng, self.sem, self.base, self.k, self.loops = eng, sem, 0, 0, 0

    def did(self, ins):
        ins.then_inc(self.sem, 1)
        self.k += 1

    def link(self, ins):
        self.did(ins)
        self.wait()

    def wait(self):
        self.eng.wait_ge(self.sem, self.base + self.k)


def steps(eng, own, first, step, last):
    first()
    if own is None:
        with eng.Fori(0, (B - 2) // 2) as j:
            step(2 * j + 1, 1)
            step(2 * j + 2, 0)
    else:
        k0, per = own.k, PER_TURN[own.loops]
        with eng.Fori(0, (B - 2) // 2) as j:
            own.base, own.k = k0 + j * per, 0
            step(2 * j + 1, 1)
            step(2 * j + 2, 0)
            assert own.k == per, own.k
        own.base, own.k = 0, k0 + (B - 2) // 2 * per
        own.loops += 1
    last()


def build(nc, x, wqkg, wv, wp, gn, log_dt, log_a, a_im, bc, cc, dd, rw, rb, w1, w3, w2,
          rope, causal, same_head, onehot, ident, lower, out):
    ctx = ExitStack()
    with ctx:
        def sem(name):
            return ctx.enter_context(nc.semaphore(name))

        def alloc(stack, name, shape, dt=F32):
            return stack.enter_context(nc.sbuf_tensor(name, shape, dt))

        bank = [ctx.enter_context(nc.psum_tensor(f"bank{i}", [P, 512], F32)) for i in range(8)]
        gate_rows = nc.dram_tensor("gate_rows", (2, P * NC * E), F32, kind="Internal").ap()

        X = alloc(ctx, "X", [P, B, NC, C])
        W1 = [alloc(ctx, f"W1{s}", [P, E, F], F32R) for s in ("hi", "lo")]
        W3 = [alloc(ctx, f"W3{s}", [P, E, F], F32R) for s in ("hi", "lo")]
        ID = alloc(ctx, "ID", [P, P])
        stats = alloc(ctx, "stats", [P, NC, 6])
        mv = alloc(ctx, "mv", [P, NC, 2])
        veps = alloc(ctx, "veps", [P, NC])
        rstd = alloc(ctx, "rstd", [P, NC])
        half = alloc(ctx, "half", [P, 16])
        warm = alloc(ctx, "warm", [P, 1])
        xn = alloc(ctx, "xn", [P, NC, C])
        xnT = alloc(ctx, "xnT", [P, T])
        RW = alloc(ctx, "RW", [P, 32])
        LT = alloc(ctx, "LT", [P, P])
        RB = alloc(ctx, "RB", [P, 1, E])
        LG = alloc(ctx, "LG", [P, NC, E])
        LD = alloc(ctx, "LD", [P, NC, E])
        LE = alloc(ctx, "LE", [P, NC, E])
        mx = alloc(ctx, "mx", [P, NC])
        GT = alloc(ctx, "GT", [P, NC, E, E])
        EQ = alloc(ctx, "EQ", [P, NC, E, E])
        LOWER = alloc(ctx, "LOWER", [P, NC, E, E])
        rank = alloc(ctx, "rank", [P, NC, E])
        pm = alloc(ctx, "pm", [P, NC, E])
        smr = alloc(ctx, "smr", [P, NC])
        G = alloc(ctx, "G", [P, NC, E])
        EULER = alloc(ctx, "EULER", [P, NS])
        xs = [[alloc(ctx, f"x{s}0", [P, T], F32R) for s in ("hi", "lo")]]
        GB = [alloc(ctx, "GB0", [P, T, E])]

        att = ExitStack()
        with att:
            QE = [alloc(att, f"QE{i}", [P, H, T]) for i in range(2)]
            Wqkg = alloc(att, "Wqkg", [P, 3, C])
            Wv = alloc(att, "Wv", [P, C])
            Wp = alloc(att, "Wp", [P, C])
            RP = alloc(att, "RP", [P, 2, NC, 2, C])
            CAUS = alloc(att, "CAUS", [P, 1, P])
            SAME = alloc(att, "SAME", [P, P])
            ONEHOT = alloc(att, "ONEHOT", [P, H])
            GN = alloc(att, "GN", [P, 2])
            qT = [alloc(att, f"qT{i}", [P, T]) for i in range(2)]
            kT = [alloc(att, f"kT{i}", [P, T]) for i in range(2)]
            QK = [alloc(att, f"QK{i}", [P, NC, 2, C]) for i in range(2)]
            V = [alloc(att, f"V{i}", [P, NC, C]) for i in range(2)]
            VE = [alloc(att, f"VE{i}", [P, NC, HG, C]) for i in range(2)]
            PR = alloc(att, "PR", [P, 8, HG, P])
            t1 = alloc(att, "t1", [P, T])
            t2 = alloc(att, "t2", [P, T])
            SG = [alloc(att, f"SG{i}", [P, T]) for i in range(2)]
            Ysb = alloc(att, "Ysb", [P, T])
            og = alloc(att, "og", [P, T])
            STsb = alloc(att, "STsb", [P, NC - 1, C])
            group = alloc(att, "group", [P, 15])
            gs6, gmv, gst, gsm = group[:, 0:6], group[:, 6:8], group[:, 8:10], group[:, 10:15]
        W1raw, W3raw = QE[0][:, 8:12, :], QE[0][:, 12:16, :]
        W2raw = VE[0][:].rearrange("p c i h -> p (c i) h")

        W2 = [alloc(ctx, f"W2{s}", [P, NCH, C], F32R) for s in ("hi", "lo")]
        hs = [[alloc(ctx, f"h{s}{i}", [P, F], F32R) for s in ("hi", "lo")] for i in range(4)]
        rows = alloc(ctx, "rows", [P, 56, NS])
        BC4 = alloc(ctx, "BC4", [P, 4, NS])
        DD = alloc(ctx, "DD", [P, 1])
        DT = alloc(ctx, "DT", [P, 1])
        L2 = alloc(ctx, "L2", [P, B, 2, NS])
        tmp = alloc(ctx, "tmp", [P, B, 2, NS])
        K = alloc(ctx, "K", [P, B])
        xs.append([alloc(ctx, f"x{s}1", [P, T], F32R) for s in ("hi", "lo")])
        hf = [alloc(ctx, f"hf{i}", [P, T]) for i in range(2)]
        sa = [alloc(ctx, f"sa{i}", [P, T]) for i in range(2)]
        oacc = alloc(ctx, "oacc", [P, T])
        otmp = alloc(ctx, "otmp", [P, T])
        GB.append(alloc(ctx, "GB1", [P, T, E]))
        xns = alloc(ctx, "xns", [P, NC, C])
        XT = alloc(ctx, "XT", [P, B, T])
        DK = alloc(ctx, "DK", [P, B, P])
        sst = alloc(ctx, "sst", [P, NC, 6])
        smv = alloc(ctx, "smv", [P, NC, 2])
        sve = alloc(ctx, "sve", [P, NC])
        srs = alloc(ctx, "srs", [P, NC])

        x_first, x_second, x_rest = sem("x_first"), sem("x_second"), sem("x_rest")
        att_in, rope_in, late_in, ffn_in, par_in = (
            sem("att_in"), sem("rope_in"), sem("late_in"), sem("ffn_in"), sem("par_in"))
        w_in = [sem(f"w_in{i}") for i in range(3)]
        half_set, zero_set, ve_zero, euler_set = (
            sem("half_set"), sem("zero_set"), sem("ve_zero"), sem("euler_set"))
        w_hi, w_lo = ([sem(f"w_{s}{i}") for i in range(3)] for s in ("hi", "lo"))
        dve_own, pool_own = sem("dve_own"), sem("pool_own")
        a_ve, a_rs, a_xn = sem("a_variance"), sem("a_rstd"), sem("a_normed")
        KINDS = {"T": 1, "qk0": 1, "qt": 1, "v": 1, "kt": 1, "gn": 0, "qk1": 0, "proj": 0, "g": 0}
        made = {kind: sem(f"made_{kind}") for kind in KINDS}
        rope_done, gn_read = sem("rope_done"), sem("gn_read")
        xnT_ready, qk_ready, qT_ready, kT_ready, v_ready, sg_ready = (
            sem("xnT_ready"), sem("qk_ready"), sem("qT_ready"), sem("kT_ready"), sem("v_ready"),
            sem("sg_ready"))
        qe_act, qe_pool, qe_dve = sem("qe_act"), sem("qe_pool"), sem("qe_dve")
        sc_ready, sc_copied, p_dve, p_pool, pv_done = (
            sem("sc_ready"), sem("sc_copied"), sem("p_dve"), sem("p_pool"), sem("pv_done"))
        st_ready, st_sb, y_sb = sem("st_ready"), sem("st_sb"), sem("y_sb")
        gm_ready, gv_ready, gr_ready, og_ready, x1_done = (
            sem("gm_ready"), sem("gv_ready"), sem("gr_ready"), sem("og_ready"), sem("x1_done"))
        k_ready, dk_ready = sem("k_ready"), sem("dk_ready")
        s_ve, s_rs, s_xn, s_T, s_xT = (
            sem("s_variance"), sem("s_rstd"), sem("s_normed"), sem("s_T"), sem("s_xT"))
        s_y, x3_done = sem("s_y"), sem("x3_done")
        stored = sem("stored")

        names = ("ve rs xn T xT hx lx lT lc lg lr ld le gates gst gld a b sa h hi lo o og os ob "
                 "xd").split()
        mix = {n: sem(f"m_{n}") for n in names}

        def read_of(kind, m):
            return {"T": (xnT_ready, m + 1), "v": (v_ready, 5 * m + 5), "kt": (kT_ready, m + 1),
                    "qk0": (rope_done, 6 * m + 3), "qk1": (rope_done, 6 * m + 6),
                    "qt": (qT_ready, m + 1), "g": (sg_ready, m + 1), "gn": (gn_read, m + 1),
                    "proj": (x1_done, m + 1)}[kind]

        def free_for(eng, kind, m):
            known = isinstance(m, int)
            before = {"qk0": "T", "qt": "qk0", "v": "qt", "kt": "v"}
            if known and m == 0:
                before |= {"v": "qk0", "qt": "v", "kt": "qt"}
            if kind in before:
                eng.wait_ge(*read_of(before[kind], m))
            elif kind == "T" and not (known and m == 0):
                eng.wait_ge(*read_of("kt", m - 1))
            elif kind == "qk1" and not (known and m < 2):
                eng.wait_ge(*read_of("gn", m - 2))
            elif kind == "qk1" and m == 1:
                eng.wait_ge(*read_of("g", 0))
            elif kind == "g":
                eng.wait_ge(*(read_of("qk1", m) if known and m < 2 else read_of("proj", m - 2)))
            elif kind == "proj":
                last = known and m >= B - 2
                eng.wait_ge(*(read_of("gn", m) if last else read_of("qk1", m + 2)))
            elif kind == "gn":
                last = known and m == B - 1
                eng.wait_ge(*(read_of("proj", m - 1) if last else read_of("g", m + 1)))
            return bank[6 + KINDS[kind]]

        def ready_for(eng, kind, m):
            eng.wait_ge(made[kind], m + 1)
            return bank[6 + KINDS[kind]]

        def wait_apart(eng, semaphore, value):
            if not isinstance(value, int):
                value = eng.to_reg(value)
                eng.wait_ge(x_first, 16)
            eng.wait_ge(semaphore, value)

        def batch(m):
            return X[:, m:m + 1] if isinstance(m, int) else X[:, bass.ds(m, 1)]

        def tiles(m):
            return [batch(m)[:, 0, c, :] for c in range(NC)]

        def beside(k, *parts):
            for part in parts:
                if k in part:
                    part[k]()

        def begun(i, n):
            return not (isinstance(i, int) and i < n)

        block = ctx.enter_context(nc.Block())

        @block.sync
        def _(sp):
            xv = x.rearrange("b (c p) h -> p b c h", p=P)
            sp.dma_start(X[:, 0], xv[:, 0]).then_inc(x_first, 16)
            for dst, src in ((ID[:], ident), (Wqkg[:], wqkg)):
                sp.dma_start(dst, src).then_inc(att_in, 16)
            for dst, src in ((RP[:], rope), (ONEHOT[:], onehot), (Wv[:], wv)):
                sp.dma_start(dst, src).then_inc(rope_in, 16)
            late = ((CAUS[:, 0], causal), (SAME[:], same_head), (Wp[:], wp),
                    (GN[:], gn))
            for dst, src in late:
                sp.dma_start(dst, src).then_inc(late_in, 16)
            assert 16 * len(late) == LATE
            sp.dma_start(X[:, 1], xv[:, 1]).then_inc(x_second, 16)
            for b in range(2, B):
                sp.dma_start(X[:, b], xv[:, b]).then_inc(x_rest, 16)
            sp.wait_ge(zero_set, 1)
            sp.dma_start(RW[:, 0:E], rw).then_inc(ffn_in, 16)
            sp.dma_start(RB[:, 0, :], rb.partition_broadcast(P)).then_inc(ffn_in, 16)
            sp.dma_start(LOWER[:], lower).then_inc(ffn_in, 16)
            sp.wait_ge(sc_ready, 16 * (B - 1))
            sp.dma_start(W1raw, w1.rearrange("e d f -> d e f")).then_inc(w_in[0], 16)
            sp.dma_start(W3raw, w3.rearrange("e d f -> d e f")).then_inc(w_in[1], 16)
            sp.wait_ge(pv_done, NC * (B - 1))
            sp.dma_start(W2raw, w2.rearrange("e (m f) d -> f (e m) d", f=P)).then_inc(w_in[2], 16)

            def gates_out(g, p):
                sp.wait_ge(mix["gates"], g + 1)
                row = gate_rows[p]
                sp.dma_start(row.rearrange("(c q e) -> q c e", c=NC, e=E), G[:])\
                    .then_inc(mix["gst"], 16)
                sp.wait_ge(mix["gst"], 16 * (g + 1))
                sp.dma_start(GB[p][:].rearrange("q t e -> q (t e)"),
                             row.partition_broadcast(P)).then_inc(mix["gld"], 16)

            def s4d_parts():
                sp.wait_ge(sc_ready, 16 * B)
                parts = ((DT[:], log_dt), (rows[:, 0], log_a), (rows[:, 1], a_im),
                         (BC4[:, 0:2], bc), (BC4[:, 2:4], cc),
                         (DD[:], dd.rearrange("(h o) -> h o", o=1)))
                for dst, src in parts:
                    sp.dma_start(dst, src).then_inc(par_in, 16)
                assert 16 * len(parts) == PARTS

            gates_out(0, 0)
            s4d_parts()
            gates_out(1, 1)
            with sp.Fori(0, B - 1) as j:
                gates_out(2 * j + 2, 0)
                gates_out(2 * j + 3, 1)
            ov = out.rearrange("b (c p) h -> p b c h", p=P)
            for b in range(B):
                sp.wait_ge(mix["xd"], B + b + 1)
                sp.dma_start(ov[:, b], X[:, b]).then_inc(stored, 16)
            sp.wait_ge(stored, 16 * B)

        @block.tensor
        def _(pe):
            def front_T(m, p):
                pe.wait_ge(a_xn, m + 1)
                ps = free_for(pe, "T", m)
                for c in range(NC):
                    mm = pe.transpose(ps[:, c * P:(c + 1) * P], xn[:, c, :], ID[:])
                mm.then_inc(made["T"], 1)

            def project_qk(m, half):
                kind = f"qk{half}"
                ps = free_for(pe, kind, m)
                pe.wait_ge(xnT_ready, m + 1)
                for i in range(NC // 2):
                    c = NC // 2 * half + i
                    mm = pe.matmul(ps[:, 2 * i * C:2 * (i + 1) * C], xnT[:, c * P:(c + 1) * P],
                                   Wqkg[:, 0:2, :], start=True, stop=True)
                mm.then_inc(made[kind], 1)

            def project_gate(m):
                ps = free_for(pe, "g", m)
                pe.matmul(ps[:], Wqkg[:, 2, :], xnT[:], start=True, stop=True).then_inc(made["g"], 1)

            def project_v(m, p):
                ps = free_for(pe, "v", m)
                for c in range(NC):
                    mm = pe.matmul(ps[:, c * P:(c + 1) * P], xnT[:, c * P:(c + 1) * P], Wv[:],
                                   start=True, stop=True)
                mm.then_inc(made["v"], 1)

            def turn_qk(kind, j, m, p):
                ps = free_for(pe, kind, m)
                pe.wait_ge(qk_ready, 2 * m + 2)
                for c in range(NC):
                    mm = pe.transpose(ps[:, c * P:(c + 1) * P], QK[p][:, c, j, :], ID[:])
                mm.then_inc(made[kind], 1)

            def scores(n, p, s):
                c, hg = divmod(s, HG)
                if c == 0:
                    if hg == 0:
                        pe.wait_ge(kT_ready, n + 1)
                    if isinstance(n, int) and n == 0:
                        here = sum(h < 4 * hg + 4 for h in FIRST_HEADS)
                        pe.wait_ge(qe_act, here)
                        pe.wait_ge(qe_dve, 4 * hg + 4 - here)
                    else:
                        pe.wait_ge(qe_act, 12 * n + 3 * hg - 3)
                        pe.wait_ge(qe_pool, 4 * (n - 1) + hg + 1)
                k = 4 * n + c
                if begun(k, 1):
                    if hg < 3:
                        pe.wait_ge(p_dve, 3 * (k - 1) + hg + 1)
                    else:
                        pe.wait_ge(sc_copied, k)
                for j in range(P // 32):
                    cols = slice(c * P + 32 * j, (c + 1) * P)
                    dst = bank[hg][32 * j:32 * j + 32, :].rearrange("s (i t) -> s i t", i=HG)
                    mm = pe.matmul(dst[:, :, 32 * j:], kT[p][:, c * P + 32 * j:c * P + 32 * j + 32],
                                   QE[p][:, 4 * hg:4 * hg + 4, cols], start=True, stop=True)
                mm.then_inc(sc_ready, 1)

            def state(n, p, c):
                if begun(3 * n + c, 1):
                    pe.wait_ge(st_sb, 3 * n + c)
                pe.matmul(bank[5][:, 0:C], QK[p][:, c, 1, :], V[p][:, c, :], start=(c == 0),
                          stop=(c == 2), skip_group_check=True).then_inc(st_ready, 1)

            def mix_v(n, p, c):
                cs = slice(c * P, (c + 1) * P)
                if c == 0 and begun(n, 1):
                    pe.wait_ge(y_sb, n)
                if c:
                    pe.wait_ge(st_sb, 3 * n + c)
                    pe.matmul(bank[4][:, cs], STsb[:, c - 1, :], qT[p][:, cs], start=True, stop=False,
                              skip_group_check=True)
                pe.wait_ge(p_dve, 12 * n + 3 * c + 3)
                pe.wait_ge(p_pool, 4 * n + c + 1)
                for i in range(HG):
                    for hg in range(HG):
                        mm = pe.matmul(bank[4][32 * hg:32 * hg + 32, cs],
                                       VE[p][:, c, i, 32 * hg:32 * hg + 32],
                                       PR[:, (4 * c + hg) % 8, i, :],
                                       start=(c == 0 and i == 0), stop=(i == HG - 1),
                                       skip_group_check=True)
                mm.then_inc(pv_done, 1)

            def group_mean(m):
                pe.wait_ge(gm_ready, m + 1)
                ps = free_for(pe, "gn", m)
                pe.matmul(ps[:, 0:2], SAME[:], gmv[:], start=True, stop=True).then_inc(made["gn"], 1)

            def project_out(m):
                pe.wait_ge(og_ready, m + 1)
                ps = free_for(pe, "proj", m)
                for c in range(NC):
                    mm = pe.matmul(ps[:, c * P:(c + 1) * P], og[:, c * P:(c + 1) * P], Wp[:],
                                   start=True, stop=True)
                mm.then_inc(made["proj"], 1)

            def step(n, p, extra={}, front=True, tail=True):
                q = 1 - p
                for s in range(16):
                    scores(n, p, s)
                    if s in (4, 7, 10):
                        state(n, p, s // 3 - 1)
                    if s == 1 and tail:
                        mix_v(n - 1, q, 3)
                    if s == 4 and tail:
                        group_mean(n - 1)
                    if s == 5:
                        if front:
                            front_T(n + 1, q)
                        mix_v(n, p, 0)
                    if s == 9:
                        mix_v(n, p, 1)
                    if s == 11 and tail:
                        project_out(n - 1)
                    if s == 13:
                        mix_v(n, p, 2)
                    if front:
                        if s in (6, 7):
                            project_qk(n + 1, s - 6)
                        if s == 10:
                            turn_qk("qt", 0, n + 1, q)
                        if s == 12:
                            project_v(n + 1, q)
                        if s == 13:
                            project_gate(n + 1)
                        if s == 14:
                            turn_qk("kt", 1, n + 1, q)
                    beside(s, extra)

            def tile_T(g):
                pe.wait_ge(mix["xn"], g + 1)
                if begun(g, 1):
                    pe.wait_ge(mix["lr"], g)
                for c in range(NC):
                    mm = pe.transpose(bank[7][:, c * P:(c + 1) * P], xn[:, c, :], ID[:])
                mm.then_inc(mix["T"], 1)

            def logits(g):
                pe.wait_ge(mix["xT"], g + 1)
                pe.wait_ge(mix["hx"], g + 1)
                for c in range(NC):
                    mm = pe.matmul(bank[7][32 * c:32 * c + 32, 0:P], RW[:],
                                   xnT[:, c * P:(c + 1) * P], start=True, stop=True)
                mm.then_inc(mix["lT"], 1)

            def turn_logits(g):
                pe.wait_ge(mix["lc"], g + 1)
                pe.transpose(bank[7][:, P:2 * P], LT[:], ID[:]).then_inc(mix["lg"], 1)

            def split_product(ps, w, cols, v, start, stop):
                for a, (i, j) in enumerate(((0, 0), (0, 1), (1, 0))):
                    mm = pe.matmul(ps[:], w[i][cols], v[j][:], start=(start and a == 0),
                                   stop=(stop and a == 2))
                return mm

            def up(g, p, k):
                e, m = divmod(k, FC)
                cols = (slice(None), e, slice(m * P, (m + 1) * P))
                i = NCH * g + k
                if begun(i, 2):
                    pe.wait_ge(mix["sa"], i - 1)
                split_product(bank[k % 2], W1, cols, xs[p], True, True).then_inc(mix["a"], 1)
                if begun(i, 2):
                    pe.wait_ge(mix["h"], i - 1)
                split_product(bank[2 + k % 2], W3, cols, xs[p], True, True).then_inc(mix["b"], 1)

            def down(g, k):
                e, m = divmod(k, FC)
                if m == 0 and begun(4 * g + e, 2):
                    pe.wait_ge(mix["og"], 4 * g + e - 1)
                pe.wait_ge(mix["lo"], NCH * g + k + 1)
                mm = split_product(bank[4 + e % 2], W2, (slice(None), k, slice(None)), hs[k % 4],
                                   m == 0, m == FC - 1)
                if m == FC - 1:
                    mm.then_inc(mix["o"], 1)

            def tile_back(g):
                pe.wait_ge(mix["os"], g + 1)
                for c in range(NC):
                    mm = pe.transpose(bank[6][:, c * P:(c + 1) * P],
                                      oacc[:, c * P:(c + 1) * P], ID[:])
                mm.then_inc(mix["ob"], 1)

            def turn(b):
                pe.wait_ge(s_xn, b + 1)
                pe.wait_ge(mix["lr"], b + 3)
                for c in range(NC):
                    mm = pe.transpose(bank[7][:, c * P:(c + 1) * P], xns[:, c, :], ID[:])
                mm.then_inc(s_T, 1)

            def convolve(b):
                pe.wait_ge(s_xT, b + 1)
                pe.wait_ge(dk_ready, b + 1)
                pe.wait_ge(mix["xd"], B - 2 if b < 2 else B - 1 if b < B - 2 else B)
                if b:
                    pe.wait_ge(x3_done, b)
                for c in range(NC):
                    cs = slice(c * P, (c + 1) * P)
                    for l in range(b + 1):
                        mm = pe.matmul(bank[6][:, cs], XT[:, b - l, cs], DK[:, l, :],
                                       start=(l == 0), stop=(l == b))
                mm.then_inc(s_y, 1)

            def front_at(g, later=0):
                return {7 + later: lambda: tile_T(g), 10: lambda: logits(g),
                        11: lambda: turn_logits(g)}

            def tail_at(g):
                return {0: lambda: down(g, NCH - 3), 1: lambda: down(g, NCH - 2),
                        2: lambda: down(g, NCH - 1), 5: lambda: tile_back(g)}

            def turn_at(b):
                return {14: lambda: turn(b)}

            def mixture_step(g, p, *others):
                pe.wait_ge(mix["lx"], g + 1)
                for k in range(NCH):
                    up(g, p, k)
                    if k >= BEHIND:
                        down(g, k - BEHIND)
                    beside(k, *others)

            def first_step(n, p):
                mixture_step(n, p, tail_at(n - 1), front_at(n + 1), turn_at(n - 1))

            def second_step(n, p):
                mixture_step(B + n, p, tail_at(B + n - 1), front_at(B + n + 1),
                             {4: lambda: pe.wait_ge(x3_done, B)})

            pe.wait_ge(half_set, 1)
            for _ in range(14):
                pe.matmul(bank[5][0:16, 0:P], half[:], half[:, 0:1].to_broadcast([P, P]),
                          start=True, stop=True)
            pe.wait_ge(att_in, 32)
            front_T(0, 0)
            project_qk(0, 0)
            project_qk(0, 1)
            pe.wait_ge(rope_in, 48)
            project_v(0, 0)
            project_gate(0)
            turn_qk("qt", 0, 0, 0)
            turn_qk("kt", 1, 0, 0)
            pe.wait_ge(ve_zero, 2)
            pe.wait_ge(v_ready, 5)
            pe.wait_ge(late_in, LATE)
            pe.wait_ge(zero_set, 1 + HG)
            steps(pe, None, lambda: step(0, 0, tail=False), step, lambda: step(B - 1, 1, {
                5: lambda: tile_T(0), 9: lambda: logits(0), 13: lambda: turn_logits(0)},
                front=False))
            pe.wait_ge(p_dve, 3 * NC * B)
            pe.wait_ge(w_lo[0], 1)
            pe.wait_ge(w_lo[1], 1)

            steps(pe, None, lambda: mixture_step(0, 0, front_at(1), {
                0: lambda: mix_v(B - 1, 1, 3), 2: lambda: (
                    pe.wait_ge(w_lo[2], 1), pe.wait_ge(y_sb, B)),
                3: lambda: group_mean(B - 1), 8: lambda: project_out(B - 1)}), first_step,
                lambda: mixture_step(B - 1, 1, {
                    1: lambda: convolve(0), 3: lambda: convolve(1),
                    5: lambda: pe.wait_ge(x3_done, 2), 8: lambda: convolve(2),
                    10: lambda: convolve(3), 12: lambda: convolve(4), 14: lambda: convolve(5)},
                    tail_at(B - 2), front_at(B, 1), turn_at(B - 2)))

            steps(pe, None, lambda: mixture_step(B, 0, tail_at(B - 1), front_at(B + 1), {
                10: lambda: convolve(B - 2), 14: lambda: turn(B - 1),
                15: lambda: convolve(B - 1)}), second_step,
                lambda: mixture_step(2 * B - 1, 1, tail_at(2 * B - 2)))
            for k in (0, 1, 2, 5):
                tail_at(2 * B - 1)[k]()

        @block.scalar
        def _(act):
            def spread_head(p, h):
                nc.scalar.activation(QE[p][:, h, :], qT[p][:], ACT.Copy,
                                     scale=ONEHOT[:, h:h + 1]).then_inc(qe_act, 1)

            def spread(m, p, k):
                if k == 0:
                    act.wait_ge(qT_ready, m + 1)
                spread_head(p, 4 * (k // 3) + (0, 2, 3)[k % 3])

            def copy_T(m):
                ps = ready_for(act, "T", m)
                nc.scalar.activation(xnT[:], ps[:], ACT.Copy).then_inc(xnT_ready, 1)

            def copy_v(m, p):
                ps = ready_for(act, "v", m)
                nc.scalar.activation(V[p][:].rearrange("p c h -> p (c h)"), ps[:], ACT.Copy)\
                    .then_inc(v_ready, 1)
                pv = ps[:].rearrange("p (c g i d) -> p c g i d", c=NC, g=HG, i=HG)
                vv = VE[p][:].rearrange("p c i (g j d) -> p c i g j d", g=HG, j=HG)
                for i in range(HG):
                    nc.scalar.activation(vv[:, :, i, :, i, :], pv[:, :, :, i, :], ACT.Copy)\
                        .then_inc(v_ready, 1)

            def gate(m, p):
                ps = ready_for(act, "g", m)
                nc.scalar.activation(SG[p][:], ps[:], ACT.Silu).then_inc(sg_ready, 1)

            def copy_qk(kind, dst, m, done):
                ps = ready_for(act, kind, m)
                nc.scalar.activation(dst[:], ps[:], ACT.Copy).then_inc(done, 1)

            def copy_scores(n, c):
                k = 4 * n + c
                if begun(k, 2):
                    act.wait_ge(pv_done, k - 1)
                act.wait_ge(sc_ready, 16 * n + 4 * c + 4)
                nc.scalar.activation(PR[:, (4 * c + 3) % 8].rearrange("p i t -> p (i t)"), bank[3][:],
                                     ACT.Copy).then_inc(sc_copied, 1)

            def read_y(m):
                act.wait_ge(pv_done, 4 * m + 4)
                nc.scalar.activation(Ysb[:], bank[4][:], ACT.Copy).then_inc(y_sb, 1)

            def step(n, p, extra={}, front=True, tail=True):
                q = 1 - p
                if tail:
                    read_y(n - 1)
                copy_scores(n, 0)
                if front:
                    copy_T(n + 1)
                beside(0, extra)
                copy_scores(n, 1)
                beside(1, extra)
                if front:
                    copy_qk("qt", qT[q], n + 1, qT_ready)
                    for k in range(3):
                        spread(n + 1, q, k)
                copy_scores(n, 2)
                beside(2, extra)
                if front:
                    for k in range(3, 6):
                        spread(n + 1, q, k)
                    copy_v(n + 1, q)
                    gate(n + 1, q)
                    spread(n + 1, q, 6)
                    copy_qk("kt", kT[q], n + 1, kT_ready)
                copy_scores(n, 3)
                if front:
                    for k in range(7, 12):
                        spread(n + 1, q, k)

            def first():
                copy_T(0)
                act.wait_ge(rope_in, 48)
                act.wait_ge(ve_zero, 2)
                copy_v(0, 0)
                copy_qk("qt", qT[0], 0, qT_ready)
                act.wait_ge(qT_ready, 1)
                for h in FIRST_HEADS:
                    spread_head(0, h)
                    if h == 0:
                        copy_qk("kt", kT[0], 0, kT_ready)
                gate(0, 0)
                step(0, 0, tail=False)

            def high(i, dst, raw):
                act.wait_ge(w_in[i], 16)
                nc.scalar.activation(dst[0][:], raw, ACT.Copy).then_inc(w_hi[i], 1)

            def mixture_front(g, p):
                act.wait_ge(mix["T"], g + 1)
                if begun(g, 1):
                    act.wait_ge(mix["lx"], g)
                    act.wait_ge(mix["lg"], g)
                nc.scalar.activation(xnT[:], bank[7][:], ACT.Copy).then_inc(mix["xT"], 1)
                if begun(g, 2):
                    act.wait_ge(mix["b"], NCH * (g - 1))
                nc.scalar.activation(xs[p][0][:], bank[7][:], ACT.Copy).then_inc(mix["hx"], 1)

            def copy_logits(g):
                act.wait_ge(mix["lT"], g + 1)
                nc.scalar.activation(LT[:], bank[7][:, 0:P], ACT.Copy).then_inc(mix["lc"], 1)

            def hidden_high(g, k):
                act.wait_ge(mix["h"], NCH * g + k + 1)
                nc.scalar.activation(hs[k % 4][0][:], hf[k % 2][:], ACT.Copy)\
                    .then_inc(mix["hi"], 1)

            def turned(b):
                act.wait_ge(s_T, b + 1)
                dst = XT[:, b, :] if isinstance(b, int) else (
                    XT[:, bass.ds(b, 1), :].rearrange("p o t -> p (o t)"))
                nc.scalar.activation(dst, bank[7][:], ACT.Copy).then_inc(s_xT, 1)

            def diagonal(l):
                act.wait_ge(k_ready, 1)
                nc.scalar.activation(DK[:, l, :], ID[:], ACT.Copy, scale=K[:, l:l + 1])\
                    .then_inc(dk_ready, 1)

            def front_at(g, p, later=0):
                return {8 + later: lambda: mixture_front(g, p), 10: lambda: copy_logits(g)}

            def tail_at(g):
                return {0: lambda: hidden_high(g, NCH - 1)}

            def turn_at(b):
                return {15: lambda: turned(b)}

            def mixture_step(g, p, *others):
                for k in range(NCH):
                    i = NCH * g + k
                    act.wait_ge(mix["a"], i + 1)
                    if begun(i, 2):
                        act.wait_ge(mix["h"], i - 1)
                    nc.scalar.activation(sa[k % 2][:], bank[k % 2][:], ACT.Silu)\
                        .then_inc(mix["sa"], 1)
                    if k:
                        hidden_high(g, k - 1)
                    beside(k, *others)

            def first_step(n, p):
                mixture_step(n, p, tail_at(n - 1), front_at(n + 1, 1 - p), turn_at(n - 1))

            def second_step(n, p):
                mixture_step(B + n, p, tail_at(B + n - 1), front_at(B + n + 1, 1 - p))

            act.wait_ge(half_set, 1)
            nc.scalar.activation(warm[:], half[:, 0:1], ACT.Silu)
            steps(act, None, first, step, lambda: step(B - 1, 1, {
                0: lambda: high(0, W1, W1raw), 1: lambda: (high(1, W3, W3raw), mixture_front(0, 0)),
                2: lambda: (copy_logits(0), high(2, W2, W2raw))}, front=False))
            read_y(B - 1)
            steps(act, None, lambda: mixture_step(0, 0, front_at(1, 1)), first_step,
                  lambda: mixture_step(B - 1, 1, tail_at(B - 2), front_at(B, 0, 1), turn_at(B - 2),
                                       {k: lambda k=k: diagonal(k) for k in range(B)}))
            steps(act, None, lambda: mixture_step(B, 0, tail_at(B - 1), front_at(B + 1, 1), {
                15: lambda: turned(B - 1)}), second_step,
                lambda: mixture_step(2 * B - 1, 1, tail_at(2 * B - 2)))
            tail_at(2 * B - 1)[0]()

        @block.vector
        def _(dve):
            own = Own(dve, dve_own)
            tt, ts = nc.vector.tensor_tensor, nc.vector.tensor_scalar
            stt = nc.vector.scalar_tensor_tensor

            def norm_stats(src, st, mv_, ve, ready):
                for c in range(NC):
                    own.did(nc.vector.bn_stats(st[:, c, :], src[c]))
                wait_apart(dve, dve_own, own.base + own.k)
                for c in range(NC):
                    own.did(nc.vector.bn_aggr(mv_[:, c, :], st[:, c, :]))
                own.wait()
                ts(ve, mv_[:, :, 1], EPS, None, ALU.add).then_inc(ready, 1)

            def norm_apply(dst, src, mv_, rs, done):
                for c in range(NC):
                    a = ts(dst[:, c, :], src[c], mv_[:, c, 0:1], rs[:, c:c + 1],
                           ALU.subtract, ALU.mult)
                a.then_inc(done, 1)

            def a_stats(m):
                if isinstance(m, int):
                    dve.wait_ge(*[(x_first, 16), (x_second, 16)][m])
                norm_stats(tiles(m), stats, mv, veps[:], a_ve)

            def a_apply(m):
                dve.wait_ge(a_rs, m + 1)
                if begun(m, 1):
                    dve.wait_ge(made["T"], m)
                norm_apply(xn, tiles(m), mv, rstd, a_xn)

            def rope(m, p, half):
                ps = ready_for(dve, f"qk{half}", m)
                if half == 0 and begun(m, 2):
                    dve.wait_ge(og_ready, m - 1)
                if half == 1:
                    dve.wait_ge(qk_ready, 2 * m + 1)
                cs = slice(NC // 2 * half, NC // 2 * (half + 1))
                v = "p (c j h two) -> p c j h two"
                tt(t1[:], ps[:], RP[:, 0, cs].rearrange("p c j h -> p (c j h)"), ALU.mult)\
                    .then_inc(rope_done, 1)
                pv = ps[:].rearrange(v, c=NC // 2, j=2, two=2)
                tv = t2[:].rearrange(v, c=NC // 2, j=2, two=2)
                sv = RP[:, 1, cs].rearrange("p c j (h two) -> p c j h two", two=2)
                for odd in (0, 1):
                    tt(tv[:, :, :, :, odd], pv[:, :, :, :, 1 - odd], sv[:, :, :, :, odd], ALU.mult)\
                        .then_inc(rope_done, 1)
                dve.wait_ge(rope_done, 6 * m + 3 * half + 3)
                tt(QK[p][:, cs].rearrange("p c j h -> p (c j h)"), t1[:], t2[:], ALU.add)\
                    .then_inc(qk_ready, 1)

            def mask(n, p, s):
                c, hg = divmod(s, HG)
                if hg == 3:
                    return
                if hg == 0 and begun(4 * n + c, 2):
                    dve.wait_ge(pv_done, 4 * n + c - 1)
                dve.wait_ge(sc_ready, 16 * n + s + 1)
                tt(PR[:, s % 8], bank[hg][:].rearrange("p (i t) -> p i t", i=HG),
                   CAUS[:].to_broadcast([P, HG, P]), ALU.mult).then_inc(p_dve, 1)

            def state(n, p, c):
                dve.wait_ge(st_ready, 3 * n + c)
                if begun(n, 1):
                    dve.wait_ge(pv_done, 4 * (n - 1) + c + 1)
                tt(STsb[:, c - 1, :], bank[5][:, 0:C], SAME[:], ALU.mult).then_inc(st_sb, 1)

            def group_a(m):
                dve.wait_ge(y_sb, m + 1)
                own.did(nc.vector.bn_stats(gs6[:], Ysb[:]))
                wait_apart(dve, dve_own, own.base + own.k)
                own.link(nc.vector.bn_aggr(gmv[:], gs6[:]))
                stt(out=gmv[:, 1:2], in0=gmv[:, 0:1], scalar=gmv[:, 0:1], in1=gmv[:, 1:2],
                    op0=ALU.mult, op1=ALU.add).then_inc(gm_ready, 1)

            def group_b(m):
                ps = ready_for(dve, "gn", m)
                ts(gst[:], ps[:, 0:2], 1.0 / HD, None, ALU.mult).then_inc(gn_read, 1)
                dve.wait_ge(gn_read, m + 1)
                own.link(stt(out=gsm[:, 0:1], in0=gst[:, 0:1], scalar=gst[:, 0:1], in1=gst[:, 1:2],
                             op0=ALU.mult, op1=ALU.subtract))
                ts(gsm[:, 1:2], gsm[:, 0:1], -1.0, EPS, ALU.mult, ALU.add).then_inc(gv_ready, 1)

            def group_c(m, p):
                dve.wait_ge(gr_ready, m + 1)
                own.link(tt(gsm[:, 3:4], gsm[:, 2:3], GN[:, 0:1], ALU.mult))
                own.link(stt(out=gsm[:, 4:5], in0=gst[:, 0:1], scalar=gsm[:, 3:4], in1=GN[:, 1:2],
                             op0=ALU.mult, op1=ALU.subtract))
                dve.wait_ge(sg_ready, m + 1)
                own.link(ts(t1[:], Ysb[:], gsm[:, 3:4], gsm[:, 4:5], ALU.mult, ALU.subtract))
                tt(og[:], t1[:], SG[p][:], ALU.mult).then_inc(og_ready, 1)

            def add_to_x(m, ps, done):
                xb = batch(m).rearrange("p o c h -> p (o c h)")
                tt(xb, ps[:], xb, ALU.add).then_inc(done, 1)

            def residual(m):
                add_to_x(m, ready_for(dve, "proj", m), x1_done)

            def step(n, p, extra={}, front=True, tail=True):
                q = 1 - p
                for s in range(16):
                    mask(n, p, s)
                    if s == 0 and front:
                        a_stats(n + 1)
                    if s in (5, 8, 11):
                        state(n, p, s // 3)
                    if s == 2 and tail:
                        group_a(n - 1)
                    if s == 3 and front:
                        a_apply(n + 1)
                    if s == 5 and tail:
                        group_b(n - 1)
                    if s == 6 and tail:
                        group_c(n - 1, q)
                    if s == 12 and tail:
                        residual(n - 1)
                    if front and s in (7, 8):
                        rope(n + 1, q, s - 7)
                    beside(s, extra)

            def first():
                a_stats(0)
                a_apply(0)
                dve.wait_ge(rope_in, 48)
                rope(0, 0, 0)
                rope(0, 0, 1)
                dve.wait_ge(qT_ready, 1)
                for h in (h for h in range(H) if h not in FIRST_HEADS):
                    ts(QE[0][:, h, :], qT[0][:], ONEHOT[:, h:h + 1], None, ALU.mult)\
                        .then_inc(qe_dve, 1)
                dve.wait_ge(late_in, LATE)
                step(0, 0, tail=False)
                dve.wait_ge(x_rest, 16 * (B - 2))

            def low_part(i, dst, raw):
                dve.wait_ge(w_hi[i], 1)
                tt(dst[1][:], raw, dst[0][:].bitcast(F32), ALU.subtract).then_inc(w_lo[i], 1)

            def m_stats(g, b):
                norm_stats(tiles(b), stats, mv, veps[:], mix["ve"])

            def m_normed(g, b):
                dve.wait_ge(mix["rs"], g + 1)
                if begun(g, 1):
                    dve.wait_ge(mix["T"], g)
                norm_apply(xn, tiles(b), mv, rstd, mix["xn"])

            def s_normed(b):
                dve.wait_ge(s_rs, b + 1)
                dve.wait_ge(mix["T"], b + 3)
                norm_apply(xns, tiles(b), smv, srs, s_xn)

            def low_x(g, p):
                dve.wait_ge(mix["hx"], g + 1)
                tt(xs[p][1][:], xnT[:], xs[p][0][:].bitcast(F32), ALU.subtract)\
                    .then_inc(mix["lx"], 1)

            def route_a(g):
                dve.wait_ge(mix["lg"], g + 1)
                tt(LG[:], bank[7][:, P:2 * P].rearrange("p (c e) -> p c e", c=NC)[:, :, 0:E],
                   RB[:].to_broadcast([P, NC, E]), ALU.add).then_inc(mix["lr"], 1)

            def route_b(g):
                dve.wait_ge(mix["lr"], g + 1)
                own.did(nc.vector.tensor_reduce(mx[:], LG[:], AX_X, ALU.max))
                lj = LG[:].unsqueeze(2).to_broadcast([P, NC, E, E])
                li = LG[:].unsqueeze(3).to_broadcast([P, NC, E, E])
                own.did(tt(GT[:], lj, li, ALU.is_gt))
                own.did(tt(EQ[:], lj, li, ALU.is_equal))

            def route_c(g):
                own.wait()
                tt(LD[:], LG[:], mx[:].unsqueeze(2).to_broadcast([P, NC, E]), ALU.subtract)\
                    .then_inc(mix["ld"], 1)
                own.did(tt(EQ[:], EQ[:], LOWER[:], ALU.mult))

            def route_d():
                own.wait()
                own.did(tt(GT[:], GT[:], EQ[:], ALU.add))

            def route_e():
                own.wait()
                own.did(nc.vector.tensor_reduce(rank[:], GT[:], AX_X, ALU.add))

            def route_f(g):
                own.wait()
                dve.wait_ge(mix["le"], g + 1)
                own.did(stt(out=pm[:], in0=rank[:], scalar=1.5, in1=LE[:],
                            op0=ALU.is_lt, op1=ALU.mult))

            def route_g(g):
                own.wait()
                own.link(nc.vector.tensor_reduce(smr[:], pm[:], AX_X, ALU.add))
                own.link(nc.vector.reciprocal(smr[:], smr[:]))
                if begun(g, 1):
                    dve.wait_ge(mix["gst"], 16 * g)
                tt(G[:], pm[:], smr[:].unsqueeze(2).to_broadcast([P, NC, E]), ALU.mult)\
                    .then_inc(mix["gates"], 1)

            def hidden(g, k):
                i = NCH * g + k
                dve.wait_ge(mix["sa"], i + 1)
                dve.wait_ge(mix["b"], i + 1)
                if begun(i, 2):
                    dve.wait_ge(mix["lo"], i - 1)
                tt(hf[k % 2][:], bank[2 + k % 2][:], sa[k % 2][:], ALU.mult)\
                    .then_inc(mix["h"], 1)

            def low(g, k):
                dve.wait_ge(mix["hi"], NCH * g + k + 1)
                tt(hs[k % 4][1][:], hf[k % 2][:], hs[k % 4][0][:].bitcast(F32), ALU.subtract)\
                    .then_inc(mix["lo"], 1)

            def gated(g, p, e):
                if e == 0:
                    dve.wait_ge(mix["gld"], 16 * (g + 1))
                    if begun(g, 1):
                        dve.wait_ge(mix["ob"], g)
                o = 4 * g + e
                dve.wait_ge(mix["o"], o + 1)
                dst = oacc if e == 0 else otmp
                tt(dst[:], bank[4 + e % 2][:], GB[p][:, :, e], ALU.mult).then_inc(mix["og"], 1)
                dve.wait_ge(mix["og"], o + 1)
                if e:
                    a = tt(oacc[:], oacc[:], otmp[:], ALU.add)
                    if e == E - 1:
                        a.then_inc(mix["os"], 1)
                    else:
                        own.did(a)

            def m_residual(g, b):
                dve.wait_ge(mix["ob"], g + 1)
                add_to_x(b, bank[6], mix["xd"])

            def s_stats(b):
                wait_apart(dve, mix["xd"], b + 1)
                norm_stats(tiles(b), sst, smv, sve[:], s_ve)

            def s_residual(b):
                dve.wait_ge(s_y, b + 1)
                add_to_x(b, bank[6], x3_done)

            def front_at(g, b, p, later=0):
                return {1 + 2 * later: lambda: m_stats(g, b), 4 + later: lambda: m_normed(g, b),
                        9 + later: lambda: low_x(g, p), 12: lambda: route_a(g),
                        13: lambda: route_b(g), 14: lambda: route_c(g)}

            def gates_at(g):
                return {0: lambda: (route_d(), route_e()), 1: lambda: route_f(g),
                        2: lambda: route_g(g)}

            def tail_at(g, b, p):
                return {0: lambda: low(g, NCH - 1), 3: lambda: gated(g, p, E - 1),
                        6: lambda: m_residual(g, b)}

            def turn_at(b):
                return {8: lambda: s_stats(b), 10: lambda: s_normed(b)}

            def mixture_step(g, p, *others):
                for k in range(NCH):
                    hidden(g, k)
                    if k:
                        low(g, k - 1)
                    if k in (7, 11, 15):
                        gated(g, p, k // 4 - 1)
                    beside(k, gates_at(g), *others)

            def first_step(n, p):
                q = 1 - p
                mixture_step(n, p, tail_at(n - 1, n - 1, q), front_at(n + 1, n + 1, q),
                             turn_at(n - 1))

            def second_step(n, p):
                q = 1 - p
                mixture_step(B + n, p, tail_at(B + n - 1, n - 1, q),
                             front_at(B + n + 1, n + 1, q))

            nc.vector.memset(half[:], -0.5).then_inc(half_set, 1)
            nc.vector.memset(RW[:], 0.0).then_inc(zero_set, 1)
            for i in range(HG):
                nc.vector.memset(bank[i][:], 0.0).then_inc(zero_set, 1)

            steps(dve, own, first, step, lambda: step(B - 1, 1, {
                0: lambda: m_stats(0, 0), 3: lambda: m_normed(0, 0), 8: lambda: low_part(1, W3, W3raw),
                10: lambda: (low_x(0, 0), dve.wait_ge(ffn_in, 48)), 14: lambda: route_a(0),
                15: lambda: route_b(0)}, front=False))
            route_c(0)
            low_part(2, W2, W2raw)
            steps(dve, own, lambda: mixture_step(0, 0, front_at(1, 1, 1), {
                0: lambda: group_a(B - 1), 4: lambda: group_b(B - 1),
                6: lambda: group_c(B - 1, 1), 9: lambda: residual(B - 1)}), first_step,
                lambda: mixture_step(B - 1, 1, {2: lambda: s_residual(0)},
                                     tail_at(B - 2, B - 2, 0), front_at(B, 0, 0, 1), turn_at(B - 2), {
                    4: lambda: s_residual(1), 9: lambda: s_residual(2), 11: lambda: s_residual(3),
                    13: lambda: s_residual(4), 15: lambda: s_residual(5)}))
            steps(dve, own, lambda: mixture_step(B, 0, tail_at(B - 1, B - 1, 1),
                                                 front_at(B + 1, 1, 1), {
                11: lambda: s_residual(B - 2), 7: lambda: s_stats(B - 1), 10: lambda: s_normed(B - 1),
                15: lambda: s_residual(B - 1)}), second_step,
                lambda: mixture_step(2 * B - 1, 1, tail_at(2 * B - 2, B - 2, 0)))
            tail = tail_at(2 * B - 1, B - 1, 1)
            for k in (0, 3, 6):
                tail[k]()

        @block.gpsimd
        def _(pool):
            own = Own(pool, pool_own)
            tt, ts = nc.gpsimd.tensor_tensor, nc.gpsimd.tensor_scalar

            def spread(m, p, hg):
                h = 4 * hg + 1
                if hg == 0:
                    wait_apart(pool, qT_ready, m + 1)
                ts(QE[p][:, h, :], qT[p][:], ONEHOT[:, h:h + 1], None, ALU.mult).then_inc(qe_pool, 1)

            def inverse_root(ready, k, out_, in_, n, done):
                pool.wait_ge(ready, k + 1)
                tt(out_, in_, half[:, 0:n], ALU.pow).then_inc(done, 1)

            def mask(n, c):
                pool.wait_ge(sc_copied, 4 * n + c + 1)
                pr = PR[:, (4 * c + 3) % 8]
                tt(pr, pr, CAUS[:].to_broadcast([P, HG, P]), ALU.mult).then_inc(p_pool, 1)

            def layer_root(m):
                inverse_root(a_ve, m, rstd[:], veps[:], NC, a_rs)

            def group_root(m):
                inverse_root(gv_ready, m, gsm[:, 2:3], gsm[:, 1:2], 1, gr_ready)

            def step(n, p, extra={}, front=True, tail=True):
                if front:
                    layer_root(n + 1)
                mask(n, 0)
                if tail:
                    group_root(n - 1)
                beside(0, extra)
                mask(n, 1)
                beside(1, extra)
                for c in (2, 3):
                    if front:
                        spread(n + 1, 1 - p, 2 * c - 4)
                    mask(n, c)
                    beside(c, extra)
                    if front:
                        spread(n + 1, 1 - p, 2 * c - 3)

            def first():
                pool.wait_ge(late_in, LATE)
                step(0, 0, tail=False)

            def kernel_terms():
                pool.wait_ge(par_in, PARTS)
                free = [2]

                def new():
                    free[0] += 1
                    return rows[:, free[0] - 1, :]

                def mul(a, b):
                    o = new()
                    own.link(tt(o, a, b, ALU.mult))
                    return o

                def add(a, b, op=ALU.add, o=None):
                    o = new() if o is None else o
                    own.link(tt(o, a, b, op))
                    return o

                def lin(a, m, c):
                    o = new()
                    own.link(ts(o, a, m, c, ALU.mult, ALU.add))
                    return o

                def exp(a):
                    o = new()
                    own.link(tt(o, EULER[:], a, ALU.pow))
                    return o

                ld = new()
                own.link(nc.gpsimd.tensor_copy(ld, DT[:].to_broadcast([P, NS])))
                dt_ = exp(ld)
                zr = lin(mul(dt_, exp(rows[:, 0, :])), -0.5, 0.0)
                zi = lin(mul(dt_, rows[:, 1, :]), 0.5, 0.0)
                one = lin(zr, -1.0, 1.0)
                zi2 = mul(zi, zi)
                den = add(mul(one, one), zi2)
                minus = lin(zr, 0.0, -1.0)
                iden = new()
                own.link(tt(iden, den, minus, ALU.pow))
                ar = mul(add(lin(mul(zr, zr), -1.0, 1.0), zi2, ALU.subtract), iden)
                ai = mul(lin(zi, 2.0, 0.0), iden)
                br, bi, cr, ci = (BC4[:, i] for i in range(4))
                pr_ = add(mul(br, cr), mul(bi, ci), ALU.subtract)
                pi_ = add(mul(br, ci), mul(bi, cr))
                w = lin(mul(dt_, iden), 0.5, 0.0)
                er, ei = mul(w, one), mul(w, zi)
                add(mul(pr_, er), mul(pi_, ei), ALU.subtract, L2[:, 0, 0, :])
                add(mul(pr_, ei), mul(pi_, er), ALU.add, L2[:, 0, 1, :])
                return ar, ai, add, mul, lin

            def kernel_powers(re, im, add, mul, lin, between):
                for k in range(3):
                    n = 1 << k
                    low, high = L2[:, 0:n], L2[:, n:2 * n]
                    rv, iv = (v.unsqueeze(1).to_broadcast([P, n, NS]) for v in (re, im))
                    u, v = tmp[:, 0:n, 0, :], tmp[:, 0:n, 1, :]
                    own.did(tt(u, low[:, :, 1, :], iv, ALU.mult))
                    own.did(tt(v, low[:, :, 1, :], rv, ALU.mult))
                    own.did(tt(high[:, :, 0, :], low[:, :, 0, :], rv, ALU.mult))
                    own.link(tt(high[:, :, 1, :], low[:, :, 0, :], iv, ALU.mult))
                    own.did(tt(high[:, :, 0, :], high[:, :, 0, :], u, ALU.subtract))
                    own.link(tt(high[:, :, 1, :], high[:, :, 1, :], v, ALU.add))
                    if k == 0:
                        between()
                    if k < 2:
                        re, im = (add(mul(re, re), mul(im, im), ALU.subtract),
                                  lin(mul(re, im), 2.0, 0.0))
                w = NS // 2
                while w:
                    own.link(tt(L2[:, :, 0, 0:w], L2[:, :, 0, 0:w], L2[:, :, 0, w:2 * w], ALU.add))
                    w //= 2
                own.did(tt(K[:, 0:1], L2[:, 0, 0, 0:1], DD[:], ALU.add))
                nc.gpsimd.tensor_copy(K[:, 1:B], L2[:, 1:B, 0, 0]).then_inc(k_ready, 1)

            def m_root(g):
                inverse_root(mix["ve"], g, rstd[:], veps[:], NC, mix["rs"])

            def s_root(b):
                inverse_root(s_ve, b, srs[:], sve[:], NC, s_rs)

            def low_part(i, dst, raw):
                pool.wait_ge(w_hi[i], 1)
                tt(dst[1][:], raw, dst[0][:].bitcast(F32), ALU.subtract).then_inc(w_lo[i], 1)

            def exps(g):
                pool.wait_ge(mix["ld"], g + 1)
                e16 = EULER[:, 0:NC * E].rearrange("p (c e) -> p c e", e=E)
                tt(LE[:], e16, LD[:], ALU.pow).then_inc(mix["le"], 1)

            def first_step(n, p):
                m_root(n + 1)
                s_root(n - 1)
                exps(n + 1)

            def second_step(n, p):
                m_root(B + n + 1)
                exps(B + n + 1)

            pool.wait_ge(half_set, 1)
            layer_root(0)
            for v in VE:
                nc.gpsimd.memset(v[:], 0.0).then_inc(ve_zero, 1)
            nc.gpsimd.memset(EULER[:], float(np.e)).then_inc(euler_set, 1)
            pool.wait_ge(euler_set, 1)
            pool.wait_ge(rope_in, 48)
            def last():
                m_root(0)
                step(B - 1, 1, {1: lambda: low_part(0, W1, W1raw), 3: lambda: exps(0)}, front=False)

            steps(pool, None, first, step, last)
            m_root(1)
            group_root(B - 1)
            terms = kernel_terms()
            kernel_powers(*terms, lambda: exps(1))
            steps(pool, None, lambda: None, first_step, lambda: (
                m_root(B), s_root(B - 2), exps(B)))
            m_root(B + 1)
            s_root(B - 1)
            exps(B + 1)
            steps(pool, None, lambda: None, second_step, lambda: None)


def launch_arrays(inputs):
    def f(name):
        return np.ascontiguousarray(inputs[name])

    w = f("L0_attn_a_w_qkv")
    q, k, v = w[0:C], w[C:2 * C], w[2 * C:]
    wqkg = np.stack([q.T, k.T, f("L0_attn_a_w_gated").T], axis=1)
    arrays = {
        "x": f("L0_attn_a_x"), "wqkg": wqkg, "wv": v.T, "wp": f("L0_attn_a_w_proj").T,
        "gn": np.stack([f("L0_attn_a_gn_weight"), f("L0_attn_a_gn_bias")], axis=1),
        "log_dt": f("L0_attn_b_log_dt"), "log_a": f("L0_attn_b_log_A_real"),
        "a_im": f("L0_attn_b_A_imag"), "bc": f("L0_attn_b_B").transpose(0, 2, 1),
        "cc": f("L0_attn_b_C").transpose(0, 2, 1), "dd": f("L0_attn_b_D"),
        "rw": f("L0_ffn_router_w"), "rb": f("L0_ffn_router_b"),
        "w1": f("L0_ffn_w1"), "w3": f("L0_ffn_w3"), "w2": f("L0_ffn_w2"),
    }
    arrays |= constants()
    return {n: np.ascontiguousarray(a) for n, a in arrays.items()}


def kernel(**inputs):
    import concourse.bacc as bacc
    from concourse.bass_utils import run_bass_kernel_spmd

    nc = bacc.Bacc("TRN2", target_bir_lowering=False, num_devices=1)
    arrays = launch_arrays(inputs)
    args = [nc.dram_tensor(n, a.shape, mybir.dt.from_np(a.dtype), kind="ExternalInput").ap()
            for n, a in arrays.items()]
    out = nc.dram_tensor("out", (B, T, C), F32, kind="ExternalOutput").ap()
    build(nc, *args, out)
    return run_bass_kernel_spmd(nc, [arrays], core_ids=[0]).results[0]["out"]
```
